# Optimizing a Trainium2 kernel written in Bass

```python
import numpy as np
import jax
import jax.numpy as jnp

def _softmax(x, axis=-1):
    return jax.nn.softmax(x, axis=axis)

def _gelu(x):
    return jax.nn.gelu(x, approximate=True)

def _silu(x):
    return jax.nn.silu(x)

def _sigmoid(x):
    return jax.nn.sigmoid(x)

def _layernorm(x, axis=-1, eps=1e-05):
    m = jnp.mean(x, axis=axis, keepdims=True)
    v = jnp.var(x, axis=axis, keepdims=True)
    return (x - m) / jnp.sqrt(v + eps)

def _scatter_add(tgt, idx, src, axis=0):
    return tgt.at[idx].add(src)

def _segment_sum(src, seg, n):
    return jax.ops.segment_sum(src, seg, n)
kernel_name = 'mk_adj_ffn_d2_adj_r2_04015f'

def setup_inputs(seed: int=0):
    np.random.seed(seed)
    _w = jnp.asarray

    def _rec_inputs():
        import jax
        import jax.numpy as jnp
        _gk = jax.random.key(seed)
        x = -0.0002928 + 1 * jax.random.normal(jax.random.fold_in(_gk, 1), (128, 128, 128), jnp.float32)
        _w = (1.0 + jnp.arange(128, dtype=jnp.float32)) ** (-0.5)
        _w = _w / _w.mean()
        _pij = jnp.clip(0.125 * _w[:, None] * _w[None, :], 0.0, 1.0)
        _a = jax.random.uniform(jax.random.fold_in(_gk, 2), (128, 128, 128)) < _pij
        _a = jnp.logical_or(_a, jnp.swapaxes(_a, -1, -2))
        _a = jnp.logical_or(_a, jnp.eye(128, dtype=bool))
        _af = _a.astype(jnp.float32)
        _af = _af * jax.random.uniform(jax.random.fold_in(_gk, 3), (128, 128, 128), jnp.float32, 0.05, 1)
        adj = _af
        return (x, adj)
    x, adj = _rec_inputs()

    def _L0_gnn_setup():
        import jax, jax.numpy as jnp
        import numpy as np
        B, N, C_IN, C_OUT = (8, 1024, 128, 128)
        key = jax.random.key(seed)
        k1, k2, k3 = jax.random.split(key, 3)
        x = jax.random.normal(k1, (B, N, C_IN), dtype=jnp.float32)
        adj = jax.random.uniform(k2, (B, N, N), dtype=jnp.float32)
        limit = float(np.sqrt(6.0 / (C_IN + C_OUT)))
        weight = jax.random.uniform(k3, (C_IN, C_OUT), minval=-limit, maxval=limit, dtype=jnp.float32)
        bias = jnp.zeros((C_OUT,), dtype=jnp.float32)
        return {'x': x, 'adj': adj, 'weight': weight, 'bias': bias}
    _L0_gnn_all = _L0_gnn_setup()
    _L0_gnn_in = {k: v for k, v in _L0_gnn_all.items() if k in ('weight', 'bias')}
    del _L0_gnn_all

    def _L0_ffn_setup():
        import jax, jax.numpy as jnp
        import numpy as np
        B, N, D = (16, 2048, 128)
        NUM_EXPERTS, TOP_K, HEADS = (4, 2, 4)
        N_EDGES = 524288
        LN_EPS = 1e-05

        def _layernorm(x, g, b):
            mu = x.mean(-1, keepdims=True)
            var = ((x - mu) ** 2).mean(-1, keepdims=True)
            return (x - mu) * jax.lax.rsqrt(var + LN_EPS) * g + b

        def _forward(x, edge_index, W_gat, att_src, att_dst, b_gat, ln_gamma, ln_beta, W1, b1, W2, b2):
            Bc, Nc, Dc = x.shape
            M = Bc * Nc
            x_flat = x.reshape(M, Dc)
            h = (x_flat @ W_gat).reshape(M, HEADS, NUM_EXPERTS)
            loops = jnp.arange(M, dtype=edge_index.dtype)
            src = jnp.concatenate([edge_index[0], loops])
            dst = jnp.concatenate([edge_index[1], loops])
            a_src = (h * att_src).sum(-1)
            a_dst = (h * att_dst).sum(-1)
            e = jax.nn.leaky_relu(a_src[src] + a_dst[dst], negative_slope=0.2)
            e_max = jax.ops.segment_max(e, dst, num_segments=M)
            ee = jnp.exp(e - e_max[dst])
            denom = jax.ops.segment_sum(ee, dst, num_segments=M)
            alpha = ee / (denom[dst] + 1e-16)
            msg = h[src] * alpha[:, :, None]
            agg = jax.ops.segment_sum(msg, dst, num_segments=M).reshape(M, HEADS * NUM_EXPERTS) + b_gat
            scores = _layernorm(agg, ln_gamma, ln_beta).reshape(M, HEADS, NUM_EXPERTS).mean(1)
            scores = scores.reshape(Bc, Nc, NUM_EXPERTS)
            topk_s, topk_i = jax.lax.top_k(scores, TOP_K)
            w = jax.nn.softmax(topk_s, axis=-1)
            out = jnp.zeros_like(x)
            for ei in range(NUM_EXPERTS):
                g = jnp.where(topk_i == ei, w, 0.0).sum(-1)
                hh = jax.nn.gelu(x @ W1[ei] + b1[ei], approximate=False)
                out = out + g[..., None] * (hh @ W2[ei] + b2[ei])
            return out
        key = jax.random.key(seed)
        ks = jax.random.split(key, 8)
        s = 0.05
        return {'x': jax.random.normal(ks[0], (B, N, D), jnp.float32), 'W_gat': jax.random.normal(ks[1], (D, HEADS * NUM_EXPERTS), jnp.float32) * s, 'att_src': jax.random.normal(ks[2], (HEADS, NUM_EXPERTS), jnp.float32) * s, 'att_dst': jax.random.normal(ks[3], (HEADS, NUM_EXPERTS), jnp.float32) * s, 'b_gat': jnp.zeros((HEADS * NUM_EXPERTS,), jnp.float32), 'ln_gamma': jnp.ones((HEADS * NUM_EXPERTS,), jnp.float32), 'ln_beta': jnp.zeros((HEADS * NUM_EXPERTS,), jnp.float32), 'W1': jax.random.normal(ks[4], (NUM_EXPERTS, D, 2 * D), jnp.float32) * s, 'b1': jnp.zeros((NUM_EXPERTS, 2 * D), jnp.float32), 'W2': jax.random.normal(ks[5], (NUM_EXPERTS, 2 * D, D), jnp.float32) * s, 'b2': jnp.zeros((NUM_EXPERTS, D), jnp.float32), 'edge_index': jax.random.randint(ks[6], (2, N_EDGES), 0, B * N, jnp.int32)}
    _L0_ffn_all = _L0_ffn_setup()
    _L0_ffn_in = {k: v for k, v in _L0_ffn_all.items() if k in ('W_gat', 'att_src', 'att_dst', 'b_gat', 'ln_gamma', 'ln_beta', 'W1', 'b1', 'W2', 'b2', 'edge_index')}
    del _L0_ffn_all

    def _L1_gnn_setup():
        import jax, jax.numpy as jnp
        import numpy as np
        D_IN = 128
        D_OUT = 128
        key = jax.random.key(seed)
        k1, k2, k3 = jax.random.split(key, 3)
        B, N = (4, 2048)
        seq = jax.random.normal(k1, (B, N, D_IN), dtype=jnp.float32)
        adj = jax.random.uniform(k2, (B, N, N), dtype=jnp.float32)
        limit = float(np.sqrt(6.0 / (D_IN + D_OUT)))
        W = jax.random.uniform(k3, (D_IN, D_OUT), dtype=jnp.float32, minval=-limit, maxval=limit)
        bias = jnp.zeros((D_OUT,), dtype=jnp.float32)
        prelu_a = jnp.array(0.25, dtype=jnp.float32)
        return {'seq': seq, 'adj': adj, 'W': W, 'bias': bias, 'prelu_a': prelu_a}
    _L1_gnn_all = _L1_gnn_setup()
    _L1_gnn_in = {k: v for k, v in _L1_gnn_all.items() if k in ('W', 'bias', 'prelu_a')}
    del _L1_gnn_all

    def _L1_ffn_setup():
        import jax, jax.numpy as jnp
        import numpy as np
        H, P, G, NS, K = (8, 64, 64, 64, 3)
        D_INNER = H * P
        CONV_DIM = D_INNER + 2 * NS
        D_IN_PROJ = 2 * D_INNER + 2 * NS + 2 * H

        def _hydra(u, in_w, conv_w, conv_b, dt_bias, A_log, Dp, fcD_w, norm_w, out_w):
            Bt, L, _ = u.shape
            zxbcdt = u @ in_w.T
            z = zxbcdt[..., :D_INNER]
            xBC = zxbcdt[..., D_INNER:D_INNER + CONV_DIM]
            dt = zxbcdt[..., -2 * H:]
            dt = jnp.concatenate([dt[..., :H], jnp.flip(dt[..., H:], axis=1)], axis=0)
            dt = jax.nn.softplus(dt + dt_bias)
            xp = jnp.pad(xBC, ((0, 0), (K - 1, 0), (0, 0)))
            xBC = sum((xp[:, k:k + L, :] * conv_w[:, k] for k in range(K))) + conv_b
            xBC = jax.nn.silu(xBC)
            x = xBC[..., :D_INNER]
            Bm = xBC[..., D_INNER:D_INNER + NS]
            Cm = xBC[..., D_INNER + NS:]
            x_og = x
            x2 = jnp.concatenate([x, jnp.flip(x, 1)], 0).reshape(2 * Bt, L, H, P)
            B2 = jnp.concatenate([Bm, jnp.flip(Bm, 1)], 0)
            C2 = jnp.concatenate([Cm, jnp.flip(Cm, 1)], 0)
            dA = jnp.exp(dt * -jnp.exp(A_log))
            dBx = jnp.einsum('blh,bln,blhp->blhpn', dt, B2, x2)

            def step(h, inp):
                dA_t, dBx_t, C_t = inp
                h = h * dA_t[:, :, None, None] + dBx_t
                return (h, jnp.einsum('bhpn,bn->bhp', h, C_t))
            h0 = jnp.zeros((2 * Bt, H, P, NS), u.dtype)
            _, ys = jax.lax.scan(step, h0, (dA.transpose(1, 0, 2), dBx.transpose(1, 0, 2, 3, 4), C2.transpose(1, 0, 2)))
            y = ys.transpose(1, 0, 2, 3).reshape(2 * Bt, L, D_INNER)
            y_fw, y_bw = (y[:Bt], jnp.flip(y[Bt:], 1))
            y = jnp.pad(y_fw[:, :-1], ((0, 0), (1, 0), (0, 0))) + jnp.pad(y_bw[:, 1:], ((0, 0), (0, 1), (0, 0)))
            y = y + x_og * jnp.repeat(x_og @ fcD_w.T + Dp, P, axis=-1)
            yg = y * jax.nn.silu(z)
            yg = yg * jax.lax.rsqrt(jnp.mean(jnp.square(yg), -1, keepdims=True) + 1e-05) * norm_w
            return yg @ out_w.T
        key = jax.random.key(seed)
        ks = jax.random.split(key, 10)
        dim, Bsz, N = (128, 4, 4096)
        s = 0.02
        return {'x': jax.random.normal(ks[0], (Bsz, N, dim), jnp.float32), 'W_fx': jax.random.normal(ks[1], (D_INNER, dim), jnp.float32) * s, 'b_fx': jnp.zeros((D_INNER,), jnp.float32), 'W_x': jax.random.normal(ks[2], (D_INNER, dim), jnp.float32) * s, 'b_x': jnp.zeros((D_INNER,), jnp.float32), 'W_slice': jax.random.normal(ks[3], (G, P), jnp.float32) * s, 'b_slice': jnp.zeros((G,), jnp.float32), 'temperature': jnp.full((1, H, 1, 1), 0.5, jnp.float32), 'hy_in_w': jax.random.normal(ks[4], (D_IN_PROJ, D_INNER), jnp.float32) * s, 'hy_conv_w': jax.random.normal(ks[5], (CONV_DIM, K), jnp.float32) * s, 'hy_conv_b': jnp.zeros((CONV_DIM,), jnp.float32), 'hy_dt_bias': jnp.log(jnp.expm1(jnp.full((H,), 0.01, jnp.float32))), 'hy_A_log': jnp.log(jnp.linspace(1.0, 16.0, H)).astype(jnp.float32), 'hy_D': jnp.ones((H,), jnp.float32), 'hy_fcD_w': jax.random.normal(ks[6], (H, D_INNER), jnp.float32) * s, 'hy_norm_w': jnp.ones((D_INNER,), jnp.float32), 'hy_out_w': jax.random.normal(ks[7], (D_INNER, D_INNER), jnp.float32) * s, 'out_w': jax.random.normal(ks[8], (dim, D_INNER), jnp.float32) * s, 'out_b': jnp.zeros((dim,), jnp.float32)}
    _L1_ffn_all = _L1_ffn_setup()
    _L1_ffn_in = {k: v for k, v in _L1_ffn_all.items() if k in ('W_fx', 'b_fx', 'W_x', 'b_x', 'W_slice', 'b_slice', 'temperature', 'hy_in_w', 'hy_conv_w', 'hy_conv_b', 'hy_dt_bias', 'hy_A_log', 'hy_D', 'hy_fcD_w', 'hy_norm_w', 'hy_out_w', 'out_w', 'out_b')}
    del _L1_ffn_all
    return {'x': x, 'adj': adj, 'L0_gnn_weight': _L0_gnn_in['weight'], 'L0_gnn_bias': _L0_gnn_in['bias'], 'L0_ffn_W_gat': _L0_ffn_in['W_gat'], 'L0_ffn_att_src': _L0_ffn_in['att_src'], 'L0_ffn_att_dst': _L0_ffn_in['att_dst'], 'L0_ffn_b_gat': _L0_ffn_in['b_gat'], 'L0_ffn_ln_gamma': _L0_ffn_in['ln_gamma'], 'L0_ffn_ln_beta': _L0_ffn_in['ln_beta'], 'L0_ffn_W1': _L0_ffn_in['W1'], 'L0_ffn_b1': _L0_ffn_in['b1'], 'L0_ffn_W2': _L0_ffn_in['W2'], 'L0_ffn_b2': _L0_ffn_in['b2'], 'L0_ffn_edge_index': _L0_ffn_in['edge_index'], 'L1_gnn_W': _L1_gnn_in['W'], 'L1_gnn_bias': _L1_gnn_in['bias'], 'L1_gnn_prelu_a': _L1_gnn_in['prelu_a'], 'L1_ffn_W_fx': _L1_ffn_in['W_fx'], 'L1_ffn_b_fx': _L1_ffn_in['b_fx'], 'L1_ffn_W_x': _L1_ffn_in['W_x'], 'L1_ffn_b_x': _L1_ffn_in['b_x'], 'L1_ffn_W_slice': _L1_ffn_in['W_slice'], 'L1_ffn_b_slice': _L1_ffn_in['b_slice'], 'L1_ffn_temperature': _L1_ffn_in['temperature'], 'L1_ffn_hy_in_w': _L1_ffn_in['hy_in_w'], 'L1_ffn_hy_conv_w': _L1_ffn_in['hy_conv_w'], 'L1_ffn_hy_conv_b': _L1_ffn_in['hy_conv_b'], 'L1_ffn_hy_dt_bias': _L1_ffn_in['hy_dt_bias'], 'L1_ffn_hy_A_log': _L1_ffn_in['hy_A_log'], 'L1_ffn_hy_D': _L1_ffn_in['hy_D'], 'L1_ffn_hy_fcD_w': _L1_ffn_in['hy_fcD_w'], 'L1_ffn_hy_norm_w': _L1_ffn_in['hy_norm_w'], 'L1_ffn_hy_out_w': _L1_ffn_in['hy_out_w'], 'L1_ffn_out_w': _L1_ffn_in['out_w'], 'L1_ffn_out_b': _L1_ffn_in['out_b']}

def reference(x, adj, L0_gnn_weight, L0_gnn_bias, L0_ffn_W_gat, L0_ffn_att_src, L0_ffn_att_dst, L0_ffn_b_gat, L0_ffn_ln_gamma, L0_ffn_ln_beta, L0_ffn_W1, L0_ffn_b1, L0_ffn_W2, L0_ffn_b2, L0_ffn_edge_index, L1_gnn_W, L1_gnn_bias, L1_gnn_prelu_a, L1_ffn_W_fx, L1_ffn_b_fx, L1_ffn_W_x, L1_ffn_b_x, L1_ffn_W_slice, L1_ffn_b_slice, L1_ffn_temperature, L1_ffn_hy_in_w, L1_ffn_hy_conv_w, L1_ffn_hy_conv_b, L1_ffn_hy_dt_bias, L1_ffn_hy_A_log, L1_ffn_hy_D, L1_ffn_hy_fcD_w, L1_ffn_hy_norm_w, L1_ffn_hy_out_w, L1_ffn_out_w, L1_ffn_out_b):
    import jax
    import jax.numpy as jnp

    def _L0_gnn_ref(x, adj, weight, bias):
        import jax, jax.numpy as jnp
        import numpy as np
        B, N, C_IN, C_OUT = (8, 1024, 128, 128)
        d_inv_sqrt = (jnp.sum(adj, axis=-1) + 1e-05) ** (-0.5)
        adj_norm = d_inv_sqrt[..., :, None] * adj * d_inv_sqrt[..., None, :]
        support = jnp.einsum('bni,io->bno', x, weight)
        return jnp.einsum('bnm,bmo->bno', adj_norm, support) + bias

    def _L0_ffn_ref(x, W_gat, att_src, att_dst, b_gat, ln_gamma, ln_beta, W1, b1, W2, b2, edge_index):
        import jax, jax.numpy as jnp
        import numpy as np
        B, N, D = (16, 2048, 128)
        NUM_EXPERTS, TOP_K, HEADS = (4, 2, 4)
        N_EDGES = 524288
        LN_EPS = 1e-05

        def _layernorm(x, g, b):
            mu = x.mean(-1, keepdims=True)
            var = ((x - mu) ** 2).mean(-1, keepdims=True)
            return (x - mu) * jax.lax.rsqrt(var + LN_EPS) * g + b

        def _forward(x, edge_index, W_gat, att_src, att_dst, b_gat, ln_gamma, ln_beta, W1, b1, W2, b2):
            Bc, Nc, Dc = x.shape
            M = Bc * Nc
            x_flat = x.reshape(M, Dc)
            h = (x_flat @ W_gat).reshape(M, HEADS, NUM_EXPERTS)
            loops = jnp.arange(M, dtype=edge_index.dtype)
            src = jnp.concatenate([edge_index[0], loops])
            dst = jnp.concatenate([edge_index[1], loops])
            a_src = (h * att_src).sum(-1)
            a_dst = (h * att_dst).sum(-1)
            e = jax.nn.leaky_relu(a_src[src] + a_dst[dst], negative_slope=0.2)
            e_max = jax.ops.segment_max(e, dst, num_segments=M)
            ee = jnp.exp(e - e_max[dst])
            denom = jax.ops.segment_sum(ee, dst, num_segments=M)
            alpha = ee / (denom[dst] + 1e-16)
            msg = h[src] * alpha[:, :, None]
            agg = jax.ops.segment_sum(msg, dst, num_segments=M).reshape(M, HEADS * NUM_EXPERTS) + b_gat
            scores = _layernorm(agg, ln_gamma, ln_beta).reshape(M, HEADS, NUM_EXPERTS).mean(1)
            scores = scores.reshape(Bc, Nc, NUM_EXPERTS)
            topk_s, topk_i = jax.lax.top_k(scores, TOP_K)
            w = jax.nn.softmax(topk_s, axis=-1)
            out = jnp.zeros_like(x)
            for ei in range(NUM_EXPERTS):
                g = jnp.where(topk_i == ei, w, 0.0).sum(-1)
                hh = jax.nn.gelu(x @ W1[ei] + b1[ei], approximate=False)
                out = out + g[..., None] * (hh @ W2[ei] + b2[ei])
            return out
        return _forward(x, edge_index, W_gat, att_src, att_dst, b_gat, ln_gamma, ln_beta, W1, b1, W2, b2)

    def _L1_gnn_ref(seq, adj, W, bias, prelu_a):
        import jax, jax.numpy as jnp
        import numpy as np
        D_IN = 128
        D_OUT = 128
        seq_fts = jnp.einsum('bnd,de->bne', seq, W)
        out = jnp.einsum('bnm,bme->bne', adj, seq_fts) + bias
        return jnp.where(out >= 0, out, prelu_a * out)

    def _L1_ffn_ref(x, W_fx, b_fx, W_x, b_x, W_slice, b_slice, temperature, hy_in_w, hy_conv_w, hy_conv_b, hy_dt_bias, hy_A_log, hy_D, hy_fcD_w, hy_norm_w, hy_out_w, out_w, out_b):
        import jax, jax.numpy as jnp
        import numpy as np
        H, P, G, NS, K = (8, 64, 64, 64, 3)
        D_INNER = H * P
        CONV_DIM = D_INNER + 2 * NS
        D_IN_PROJ = 2 * D_INNER + 2 * NS + 2 * H

        def _hydra(u, in_w, conv_w, conv_b, dt_bias, A_log, Dp, fcD_w, norm_w, out_w):
            Bt, L, _ = u.shape
            zxbcdt = u @ in_w.T
            z = zxbcdt[..., :D_INNER]
            xBC = zxbcdt[..., D_INNER:D_INNER + CONV_DIM]
            dt = zxbcdt[..., -2 * H:]
            dt = jnp.concatenate([dt[..., :H], jnp.flip(dt[..., H:], axis=1)], axis=0)
            dt = jax.nn.softplus(dt + dt_bias)
            xp = jnp.pad(xBC, ((0, 0), (K - 1, 0), (0, 0)))
            xBC = sum((xp[:, k:k + L, :] * conv_w[:, k] for k in range(K))) + conv_b
            xBC = jax.nn.silu(xBC)
            x = xBC[..., :D_INNER]
            Bm = xBC[..., D_INNER:D_INNER + NS]
            Cm = xBC[..., D_INNER + NS:]
            x_og = x
            x2 = jnp.concatenate([x, jnp.flip(x, 1)], 0).reshape(2 * Bt, L, H, P)
            B2 = jnp.concatenate([Bm, jnp.flip(Bm, 1)], 0)
            C2 = jnp.concatenate([Cm, jnp.flip(Cm, 1)], 0)
            dA = jnp.exp(dt * -jnp.exp(A_log))
            dBx = jnp.einsum('blh,bln,blhp->blhpn', dt, B2, x2)

            def step(h, inp):
                dA_t, dBx_t, C_t = inp
                h = h * dA_t[:, :, None, None] + dBx_t
                return (h, jnp.einsum('bhpn,bn->bhp', h, C_t))
            h0 = jnp.zeros((2 * Bt, H, P, NS), u.dtype)
            _, ys = jax.lax.scan(step, h0, (dA.transpose(1, 0, 2), dBx.transpose(1, 0, 2, 3, 4), C2.transpose(1, 0, 2)))
            y = ys.transpose(1, 0, 2, 3).reshape(2 * Bt, L, D_INNER)
            y_fw, y_bw = (y[:Bt], jnp.flip(y[Bt:], 1))
            y = jnp.pad(y_fw[:, :-1], ((0, 0), (1, 0), (0, 0))) + jnp.pad(y_bw[:, 1:], ((0, 0), (0, 1), (0, 0)))
            y = y + x_og * jnp.repeat(x_og @ fcD_w.T + Dp, P, axis=-1)
            yg = y * jax.nn.silu(z)
            yg = yg * jax.lax.rsqrt(jnp.mean(jnp.square(yg), -1, keepdims=True) + 1e-05) * norm_w
            return yg @ out_w.T
        B, N, _ = x.shape
        fx = (x @ W_fx.T + b_fx).reshape(B, N, H, P).transpose(0, 2, 1, 3)
        xm = (x @ W_x.T + b_x).reshape(B, N, H, P).transpose(0, 2, 1, 3)
        temp = jnp.maximum(temperature, 1e-06)
        sw = jax.nn.softmax((xm @ W_slice.T + b_slice) / temp, axis=-1)
        snorm = sw.sum(2)
        st = jnp.einsum('bhnc,bhng->bhgc', fx, sw) / (snorm + 1e-05)[..., None]
        st = st.transpose(0, 2, 1, 3).reshape(B, G, D_INNER)
        ot = _hydra(st, hy_in_w, hy_conv_w, hy_conv_b, hy_dt_bias, hy_A_log, hy_D, hy_fcD_w, hy_norm_w, hy_out_w)
        ot = ot.reshape(B, G, H, P).transpose(0, 2, 1, 3)
        out = jnp.einsum('bhgc,bhng->bhnc', ot, sw).transpose(0, 2, 1, 3).reshape(B, N, D_INNER)
        return out @ out_w.T + out_b
    x = x + _L0_gnn_ref(_layernorm(x, axis=-1), adj, L0_gnn_weight, L0_gnn_bias)
    x = x + _L0_ffn_ref(_layernorm(x, axis=-1), L0_ffn_W_gat, L0_ffn_att_src, L0_ffn_att_dst, L0_ffn_b_gat, L0_ffn_ln_gamma, L0_ffn_ln_beta, L0_ffn_W1, L0_ffn_b1, L0_ffn_W2, L0_ffn_b2, L0_ffn_edge_index)
    x = x + _L1_gnn_ref(_layernorm(x, axis=-1), adj, L1_gnn_W, L1_gnn_bias, L1_gnn_prelu_a)
    x = x + _L1_ffn_ref(_layernorm(x, axis=-1), L1_ffn_W_fx, L1_ffn_b_fx, L1_ffn_W_x, L1_ffn_b_x, L1_ffn_W_slice, L1_ffn_b_slice, L1_ffn_temperature, L1_ffn_hy_in_w, L1_ffn_hy_conv_w, L1_ffn_hy_conv_b, L1_ffn_hy_dt_bias, L1_ffn_hy_A_log, L1_ffn_hy_D, L1_ffn_hy_fcD_w, L1_ffn_hy_norm_w, L1_ffn_hy_out_w, L1_ffn_out_w, L1_ffn_out_b)
    return x

_drawn_inputs = setup_inputs


def setup_inputs(seed=0):
    import zlib

    import numpy as np

    out = dict(_drawn_inputs(seed))
    spreads = {'L0_gnn_bias': (0.0, 0.1),
     'L0_ffn_b_gat': (0.0, 0.1),
     'L0_ffn_ln_gamma': (1.0, 0.2),
     'L0_ffn_ln_beta': (0.0, 0.1),
     'L0_ffn_b1': (0.0, 0.1),
     'L0_ffn_b2': (0.0, 0.1),
     'L1_gnn_bias': (0.0, 0.354),
     'L1_ffn_b_fx': (0.0, 0.32),
     'L1_ffn_b_x': (0.0, 2.0),
     'L1_ffn_b_slice': (0.0, 2.0),
     'L1_ffn_temperature': (0.5, 0.6),
     'L1_ffn_hy_conv_b': (0.0, 0.1),
     'L1_ffn_hy_dt_bias': (-4.600166320800781, 0.6),
     'L1_ffn_hy_D': (1.0, 0.6),
     'L1_ffn_hy_norm_w': (1.0, 0.6),
     'L1_ffn_out_b': (0.0, 0.1)}
    factors = {'L0_ffn_att_src': 2.961,
     'L0_ffn_att_dst': 4.664,
     'L1_ffn_W_x': 8.0,
     'L1_ffn_W_slice': 8.0,
     'L1_ffn_hy_conv_w': 8.0,
     'L1_ffn_hy_A_log': 64.0,
     'L1_ffn_hy_fcD_w': 64.0}
    for name, (base, spread) in spreads.items():
        noise = np.random.default_rng([zlib.crc32(name.encode()), seed]).standard_normal(out[name].shape)
        drawn = base * np.exp(spread * noise) if base else spread * noise
        out[name] = jnp.asarray(drawn.astype(out[name].dtype))
    for name, factor in factors.items():
        out[name] = (out[name] * factor).astype(out[name].dtype)
    return out
```

```python
from contextlib import ExitStack

import concourse.bass as bass
from concourse import mybir

ALU = mybir.AluOpType
ACT = mybir.ActivationFunctionType
F32 = mybir.dt.float32
BF16 = mybir.dt.bfloat16
I32 = mybir.dt.int32
U32 = mybir.dt.uint32
AX_X = mybir.AxisListType.X
AX_XY = mybir.AxisListType.XY
RMAX = bass.bass_isa.ReduceOp.max

P = 128
QUAD = 4
R = 4
LN_EPS = 1e-5
DEGREE_EPS = 1e-5


class Chain:

    def __init__(self, nc, ctx, eng, name, per_unit, sem=None):
        self.sem = sem or ctx.enter_context(nc.semaphore(name))
        self.eng, self.per_unit = eng, per_unit

    def unit(self, g):
        self.base, self.k = g * self.per_unit, 0

    def link(self, instruction):
        self.k += 1
        assert self.k <= self.per_unit
        instruction.then_inc(self.sem, 1)
        self.eng.wait_ge(self.sem, self.base + self.k)

    def end(self):
        assert self.k == self.per_unit, (self.k, self.per_unit)


def sweep(eng, units, parts):
    assert units % R == 0 and all(lag <= R for lag, _ in parts)
    for t in range(R):
        for lag, part in parts:
            if t >= lag:
                part(0, t - lag)
    if units > R:
        with eng.Fori(1, units // R) as q:
            for u in range(R):
                for lag, part in parts:
                    part(q + (u - lag) // R, (u - lag) % R)
    for t in range(units, units + R):
        for lag, part in parts:
            if t - lag < units:
                part((t - lag) // R, (t - lag) % R)


def before(eng, sem, q, u, back, each=1):
    if isinstance(q, int):
        n = q * R + u - back + 1
        if n > 0:
            eng.wait_ge(sem, n * each)
    else:
        eng.wait_ge(sem, (q * R + (u - back + 1)) * each)


def slot_ready(eng, sems, q, u, back=0):
    if isinstance(q, int):
        if q + 1 - back > 0:
            eng.wait_ge(sems[u], 16 * (q + 1 - back))
    else:
        eng.wait_ge(sems[u], (q + (1 - back)) * 16)


def queue_sem(nc, name):
    return nc.alloc_semaphore(name)


def clear(nc, sems):
    with nc.Block() as block:
        @block.gpsimd
        def _(pool):
            for s in sems:
                pool.sem_clear(s)


def merge_statistics(nc, steps, stats, mean, var, halves):
    nc.vector.tensor_tensor(halves[:, 0], stats[:, :, 1], stats[:, :, 4], ALU.add)
    nc.vector.tensor_tensor(halves[:, 1], stats[:, :, 1], stats[:, :, 4], ALU.subtract)
    steps.link(nc.vector.tensor_tensor(halves[:, 2], stats[:, :, 2], stats[:, :, 5], ALU.add))
    nc.vector.tensor_scalar(mean, halves[:, 0], 0.5, None, ALU.mult)
    steps.link(nc.vector.scalar_tensor_tensor(out=var, in0=halves[:, 1], scalar=0.25, in1=halves[:, 1],
                                              op0=ALU.mult, op1=ALU.mult))
    steps.link(nc.vector.scalar_tensor_tensor(out=var, in0=halves[:, 2], scalar=1.0 / P, in1=var,
                                              op0=ALU.mult, op1=ALU.add))


def gnn_stage(nc, name, ident, x_in, x_out, adj, weight, bias, prelu_a, normalize):
    graphs = adj.shape[0]
    units = graphs // QUAD
    with ExitStack() as ctx:
        sb = lambda n, shape, dt=F32: ctx.enter_context(nc.sbuf_tensor(f"{name}_{n}", shape, dt))
        pb = lambda n, shape, dt=F32: ctx.enter_context(nc.psum_tensor(f"{name}_{n}", shape, dt))
        sem = lambda n: ctx.enter_context(nc.semaphore(f"{name}_{n}"))

        w_sb = sb("w", [P, P])
        bias_b = sb("bias_b", [P, P])
        slope_b = sb("slope_b", [P, 1])
        x_sb = sb("x", [P, R, QUAD, P])
        adj_sb = sb("adj", [P, R, QUAD, P])
        stats = sb("stats", [P, R, QUAD, 6])
        halves = sb("halves", [P, R, 3, QUAD])
        mean = sb("mean", [P, R, QUAD])
        var = sb("var", [P, R, QUAD])
        deg = sb("deg", [P, R, QUAD])
        roots = 2 * QUAD if normalize else QUAD
        root_in = sb("root_in", [P, R, roots])
        root = sb("root", [P, R, roots])
        inv = sb("inv", [P, R, roots])
        scale = sb("scale", [P, R, QUAD])
        xs = sb("xs", [P, R, QUAD, P])
        adjT = sb("adjT", [P, R, QUAD, P])
        yT = sb("yT", [P, R, QUAD, P])
        act_out = sb("act_out", [P, R, QUAD, P])
        neg_out = sb("neg_out", [P, R, QUAD, P])
        xo = sb("xo", [P, R, QUAD, P])
        adjT_ps = pb("adjT_ps", [P, 2, QUAD, P])
        yT_ps = pb("yT_ps", [P, 2, QUAD, P])
        out_ps = pb("out_ps", [P, 2, QUAD, P])

        weights_loaded = sem("weights_loaded")
        x_loaded = [sem(f"x_loaded{s}") for s in range(R)]
        adj_loaded = [sem(f"adj_loaded{s}") for s in range(R)]
        x_stored = [queue_sem(nc, f"{name}_x_stored{s}") for s in range(R)]
        root_asked = sem("root_asked")
        root_ready = sem("root_ready")
        xs_ready = sem("xs_ready")
        adjT_in_psum = sem("adjT_in_psum")
        adjT_ready = sem("adjT_ready")
        yT_in_psum = sem("yT_in_psum")
        yT_ready = sem("yT_ready")
        out_in_psum = sem("out_in_psum")
        x_done = sem("x_done")

        x_rows = x_in.rearrange("(g j) n f -> g n j f", j=QUAD)
        xo_rows = x_out.rearrange("(g j) n f -> g n j f", j=QUAD)
        adj_rows = adj.rearrange("(g j) n m -> g n j m", j=QUAD)
        n_weights = 16 * (2 if normalize else 3)

        with nc.Block() as block:
            @block.sync
            def _(sp):
                sp.dma_start(w_sb[:, :], weight).then_inc(weights_loaded, 16)
                sp.dma_start(bias_b[:, :], bias.partition_broadcast(P)).then_inc(weights_loaded, 16)
                if not normalize:
                    sp.dma_start(slope_b[:, :], prelu_a.partition_broadcast(P)).then_inc(weights_loaded, 16)

                def load(q, u):
                    before(sp, x_done, q, u, R)
                    sp.dma_start(x_sb[:, u], x_rows[q * R + u]).then_inc(x_loaded[u], 16)
                    before(sp, adjT_in_psum, q, u, R)
                    before(sp, xs_ready, q, u, R)
                    sp.dma_start(adj_sb[:, u], adj_rows[q * R + u]).then_inc(adj_loaded[u], 16)

                sweep(sp, units, [(0, load)])

            @block.gpsimd
            def _(pool):
                def store(q, u):
                    before(pool, x_done, q, u, 0)
                    pool.dma_start(xo_rows[q * R + u], xo[:, u]).then_inc(x_stored[u], 16)

                sweep(pool, units, [(0, store)])
                for s in range(R):
                    pool.wait_ge(x_stored[s], 16 * (units // R))

            @block.tensor
            def _(pe):
                pe.wait_ge(weights_loaded, n_weights)

                def transpose_adj(q, u):
                    slot_ready(pe, adj_loaded, q, u)
                    before(pe, adjT_ready, q, u, 2)
                    for j in range(QUAD):
                        last = nc.tensor.transpose(adjT_ps[:, u % 2, j], adj_sb[:, u, j], ident[:, :])
                    last.then_inc(adjT_in_psum, 1)

                def aggregate(q, u):
                    before(pe, xs_ready, q, u, 0)
                    before(pe, adjT_ready, q, u, 0)
                    before(pe, yT_ready, q, u, 2)
                    for j in range(QUAD):
                        last = nc.tensor.matmul(yT_ps[:, u % 2, j], xs[:, u, j], adjT[:, u, j], start=True, stop=True)
                    last.then_inc(yT_in_psum, 1)

                def project(q, u):
                    before(pe, yT_ready, q, u, 0)
                    before(pe, x_done, q, u, 2)
                    for j in range(QUAD):
                        last = nc.tensor.matmul(out_ps[:, u % 2, j], yT[:, u, j], w_sb[:, :], start=True, stop=True)
                    last.then_inc(out_in_psum, 1)

                sweep(pe, units, [(0, transpose_adj), (1, aggregate), (2, project)])

            @block.scalar
            def _(act):
                def copy_adjT(q, u):
                    before(act, adjT_in_psum, q, u, 0)
                    before(act, yT_in_psum, q, u, R)
                    nc.scalar.copy(adjT[:, u], adjT_ps[:, u % 2]).then_inc(adjT_ready, 1)

                def copy_yT(q, u):
                    before(act, yT_in_psum, q, u, 0)
                    before(act, out_in_psum, q, u, R)
                    nc.scalar.copy(yT[:, u], yT_ps[:, u % 2]).then_inc(yT_ready, 1)

                def take_root(q, u):
                    before(act, root_asked, q, u, 0)
                    before(act, xs_ready, q, u, R)
                    nc.scalar.activation(root[:, u], root_in[:, u], ACT.Sqrt).then_inc(root_ready, 1)

                sweep(act, units, [(0, copy_adjT), (0, take_root), (1, copy_yT)])

            @block.vector
            def _(dve):
                dve.wait_ge(weights_loaded, n_weights)
                stat_steps = Chain(nc, ctx, dve, f"{name}_stat_steps", 5 if normalize else 4)
                scale_steps = Chain(nc, ctx, dve, f"{name}_scale_steps", 2 if normalize else 1)
                sum_steps = Chain(nc, ctx, dve, f"{name}_sum_steps", 1 if normalize else 3)

                def statistics(q, u):
                    stat_steps.unit(q * R + u)
                    slot_ready(dve, x_loaded, q, u)
                    slot_ready(dve, adj_loaded, q, u)
                    for j in range(QUAD):
                        last = nc.vector.bn_stats(stats[:, u, j], x_sb[:, u, j])
                    stat_steps.link(last)
                    merge_statistics(nc, stat_steps, stats[:, u], mean[:, u], var[:, u], halves[:, u])
                    if normalize:
                        stat_steps.link(nc.vector.tensor_reduce(deg[:, u], adj_sb[:, u], AX_X, ALU.add))
                        nc.vector.tensor_scalar(root_in[:, u, QUAD:2 * QUAD], deg[:, u], DEGREE_EPS, None, ALU.add)
                    stat_steps.end()
                    nc.vector.tensor_scalar(root_in[:, u, 0:QUAD], var[:, u], LN_EPS, None,
                                            ALU.add).then_inc(root_asked, 1)

                def scale_x(q, u):
                    scale_steps.unit(q * R + u)
                    before(dve, root_ready, q, u, 0)
                    scale_steps.link(nc.vector.reciprocal(inv[:, u], root[:, u]))
                    rstd = inv[:, u, 0:QUAD]
                    if normalize:
                        scale_steps.link(nc.vector.tensor_tensor(scale[:, u], inv[:, u, 0:QUAD],
                                                                 inv[:, u, QUAD:2 * QUAD], ALU.mult))
                        rstd = scale[:, u]
                    scale_steps.end()
                    before(dve, yT_in_psum, q, u, R)
                    for j in range(QUAD):
                        last = nc.vector.tensor_scalar(xs[:, u, j], x_sb[:, u, j], mean[:, u, j:j + 1],
                                                       rstd[:, j:j + 1], ALU.subtract, ALU.mult)
                    last.then_inc(xs_ready, 1)

                def add(q, u):
                    sum_steps.unit(q * R + u)
                    before(dve, out_in_psum, q, u, 0)
                    slot_ready(dve, x_stored, q, u, 1)
                    if normalize:
                        for j in range(QUAD):
                            last = nc.vector.scalar_tensor_tensor(
                                out=act_out[:, u, j], in0=out_ps[:, u % 2, j], scalar=inv[:, u, QUAD + j:QUAD + j + 1],
                                in1=bias_b[:, :], op0=ALU.mult, op1=ALU.add)
                        sum_steps.link(last)
                    else:
                        sum_steps.link(nc.vector.tensor_tensor(
                            neg_out[:, u], out_ps[:, u % 2],
                            bias_b[:, :].unsqueeze(1).to_broadcast([P, QUAD, P]), ALU.add))
                        sum_steps.link(nc.vector.tensor_scalar(act_out[:, u], neg_out[:, u], 0.0, slope_b[:, 0:1],
                                                               ALU.min, ALU.mult))
                        sum_steps.link(nc.vector.scalar_tensor_tensor(
                            out=act_out[:, u], in0=neg_out[:, u], scalar=0.0, in1=act_out[:, u],
                            op0=ALU.max, op1=ALU.add))
                    sum_steps.end()
                    nc.vector.tensor_tensor(xo[:, u], act_out[:, u], x_sb[:, u], ALU.add).then_inc(x_done, 1)

                sweep(dve, units, [(0, statistics), (1, scale_x), (3, add)])


HEADS = 4
EXPERTS = 4
HE = HEADS * EXPERTS
FEATS = HEADS * (EXPERTS + 1)
ROW = FEATS + HEADS
NODE_ROW = ROW + HEADS
TILES = 18
CHUNK = TILES * P
GROUP = 4
LEVELS = 32
LEVEL_STEP = 32.0
NEG_SLOPE = 0.2


def table_stage(nc, ident, x_in, w_gat, att_src, att_dst, node_rows, table):
    graphs = x_in.shape[0]
    units = graphs // QUAD
    PROJ = HE + 2 * HEADS
    with ExitStack() as ctx:
        sb = lambda n, shape, dt=F32: ctx.enter_context(nc.sbuf_tensor(f"tab_{n}", shape, dt))
        pb = lambda n, shape, dt=F32: ctx.enter_context(nc.psum_tensor(f"tab_{n}", shape, dt))
        sem = lambda n: ctx.enter_context(nc.semaphore(f"tab_{n}"))
        wg = sb("wg", [P, PROJ])
        att = sb("att", [P, 2, HE])
        wa = sb("wa", [P, 2, HE])
        x_sb = sb("x", [P, R, QUAD, P])
        stats = sb("stats", [P, R, QUAD, 6])
        halves = sb("halves", [P, R, 3, QUAD])
        mean = sb("mean", [P, R, QUAD])
        var = sb("var", [P, R, QUAD])
        root_in = sb("root_in", [P, R, QUAD])
        root = sb("root", [P, R, QUAD])
        inv = sb("inv", [P, R, QUAD])
        xn = sb("xn", [P, R, QUAD, P])
        xnT = sb("xnT", [P, R, QUAD, P])
        xnT_ps = pb("xnT_ps", [P, 2, QUAD, P])
        rows_ps = pb("rows_ps", [P, 2, 512])

        weights_loaded = sem("weights_loaded")
        attention_folded = sem("attention_folded")
        x_loaded = [sem(f"x_loaded{s}") for s in range(R)]
        root_asked = sem("root_asked")
        root_ready = sem("root_ready")
        xn_ready = sem("xn_ready")
        xnT_in_psum = sem("xnT_in_psum")
        xnT_ready = sem("xnT_ready")
        rows_in_psum = sem("rows_in_psum")
        rows_ready = sem("rows_ready")
        table_stored = sem("table_stored")
        x_rows = x_in.rearrange("(g j) n f -> g n j f", j=QUAD)

        with nc.Block() as block:
            @block.sync
            def _(sp):
                sp.dma_start(wg[:, 0:HE], w_gat).then_inc(weights_loaded, 16)
                sp.dma_start(att[:, 0], att_src.rearrange("h e -> (h e)").partition_broadcast(P)).then_inc(weights_loaded, 16)
                sp.dma_start(att[:, 1], att_dst.rearrange("h e -> (h e)").partition_broadcast(P)).then_inc(weights_loaded, 16)

                def load(q, u):
                    before(sp, xn_ready, q, u, R)
                    sp.dma_start(x_sb[:, u], x_rows[q * R + u]).then_inc(x_loaded[u], 16)

                sweep(sp, units, [(0, load)])
                sp.wait_ge(rows_ready, units)
                sp.dma_start(table.rearrange("(g n) c -> n g c", n=P), node_rows[:, :, 0:ROW]).then_inc(table_stored, 16)
                sp.wait_ge(table_stored, 16)

            @block.scalar
            def _(act):
                def take_root(q, u):
                    before(act, root_asked, q, u, 0)
                    before(act, xn_ready, q, u, R)
                    nc.scalar.activation(root[:, u], root_in[:, u], ACT.Sqrt).then_inc(root_ready, 1)

                def copy_xnT(q, u):
                    before(act, xnT_in_psum, q, u, 0)
                    before(act, rows_in_psum, q, u, R)
                    nc.scalar.copy(xnT[:, u], xnT_ps[:, u % 2]).then_inc(xnT_ready, 1)

                sweep(act, units, [(0, take_root), (1, copy_xnT)])

            @block.tensor
            def _(pe):
                def transpose_xn(q, u):
                    before(pe, xn_ready, q, u, 0)
                    before(pe, xnT_ready, q, u, 2)
                    for j in range(QUAD):
                        last = nc.tensor.transpose(xnT_ps[:, u % 2, j], xn[:, u, j], ident[:, :])
                    last.then_inc(xnT_in_psum, 1)

                def project(q, u):
                    before(pe, xnT_ready, q, u, 0)
                    before(pe, rows_ready, q, u, 2)
                    for j in range(QUAD):
                        last = nc.tensor.matmul(rows_ps[:, u % 2, j * PROJ:(j + 1) * PROJ], xnT[:, u, j],
                                                wg[:, :], start=True, stop=True)
                    last.then_inc(rows_in_psum, 1)

                pe.wait_ge(attention_folded, 3)
                sweep(pe, units, [(0, transpose_xn), (1, project)])

            @block.vector
            def _(dve):
                dve.wait_ge(weights_loaded, 48)
                for k in range(2):
                    last = nc.vector.tensor_tensor(wa[:, k], wg[:, 0:HE], att[:, k], ALU.mult)
                last.then_inc(attention_folded, 1)
                dve.wait_ge(attention_folded, 1)
                for k in range(2):
                    nc.vector.tensor_reduce(wg[:, HE + k * HEADS:HE + (k + 1) * HEADS],
                                            wa[:, k].rearrange("p (h e) -> p h e", h=HEADS), AX_X,
                                            ALU.add).then_inc(attention_folded, 1)
                stat_steps = Chain(nc, ctx, dve, "tab_stat_steps", 4)
                scale_steps = Chain(nc, ctx, dve, "tab_scale_steps", 1)

                def statistics(q, u):
                    stat_steps.unit(q * R + u)
                    slot_ready(dve, x_loaded, q, u)
                    for j in range(QUAD):
                        last = nc.vector.bn_stats(stats[:, u, j], x_sb[:, u, j])
                    stat_steps.link(last)
                    merge_statistics(nc, stat_steps, stats[:, u], mean[:, u], var[:, u], halves[:, u])
                    stat_steps.end()
                    nc.vector.tensor_scalar(root_in[:, u], var[:, u], LN_EPS, None, ALU.add).then_inc(root_asked, 1)

                def scale_x(q, u):
                    scale_steps.unit(q * R + u)
                    before(dve, root_ready, q, u, 0)
                    scale_steps.link(nc.vector.reciprocal(inv[:, u], root[:, u]))
                    before(dve, xnT_in_psum, q, u, R)
                    for j in range(QUAD):
                        last = nc.vector.tensor_scalar(xn[:, u, j], x_sb[:, u, j], mean[:, u, j:j + 1],
                                                       inv[:, u, j:j + 1], ALU.subtract, ALU.mult)
                    last.then_inc(xn_ready, 1)

                def keep_rows(q, u):
                    before(dve, rows_in_psum, q, u, 0)
                    rows = node_rows[:, bass.ds((q * R + u) * QUAD, QUAD), :]
                    got = rows_ps[:, u % 2, 0:QUAD * PROJ].rearrange("p (j c) -> p j c", j=QUAD)
                    nc.vector.tensor_copy(
                        rows[:, :, 0:FEATS].rearrange("p j (h c) -> p j h c", h=HEADS)[:, :, :, 0:EXPERTS],
                        got[:, :, 0:HE].rearrange("p j (h c) -> p j h c", h=HEADS))
                    nc.vector.tensor_copy(rows[:, :, FEATS:NODE_ROW], got[:, :, HE:PROJ]).then_inc(rows_ready, 1)

                nc.vector.memset(node_rows[:, :, :], 1.0).then_inc(attention_folded, 1)
                dve.wait_ge(attention_folded, 4)
                sweep(dve, units, [(0, statistics), (1, scale_x), (3, keep_rows)])



SORT_TILES = 16
SORT_GROUPS = SORT_TILES // GROUP


def max_chunks_of(n_edges, n_nodes):
    n = n_edges // CHUNK + n_nodes // P
    return n + n % 2


def sort_stage(nc, edge_index, n_nodes, sorted_edges, chunk_block, pair_count):
    n_edges = edge_index.shape[1]
    tiles = n_edges // P
    units = tiles // SORT_TILES
    slots = sorted_edges.shape[0]
    max_chunks = chunk_block.shape[1]
    block_chunks = n_edges // CHUNK + 1
    FILLS = 4
    INVALID = float(1 << 22)
    assert n_nodes // P == P and slots < INVALID and slots % (FILLS * P) == 0
    with ExitStack() as ctx:
        sb = lambda n, shape, dt=F32: ctx.enter_context(nc.sbuf_tensor(f"sort_{n}", shape, dt))
        pb = lambda n, shape, dt=F32: ctx.enter_context(nc.psum_tensor(f"sort_{n}", shape, dt))
        sem = lambda n: ctx.enter_context(nc.semaphore(f"sort_{n}"))
        src = sb("src", [P, tiles], I32)
        dst = sb("dst", [P, tiles], I32)
        src_f = sb("src_f", [P, tiles])
        work_i = sb("work_i", [P, tiles], I32)
        blk = sb("blk", [P, tiles])
        payload = sb("payload", [P, tiles, 2], I32)
        shift = sb("shift", [P, tiles])
        fill = sb("fill", [P, slots // (FILLS * P), 2], I32)
        iota_i = sb("iota_i", [P, 512], I32)
        iota_f = sb("iota_f", [P, 512])
        row_i = sb("row_i", [P, 1], I32)
        row_f = sb("row_f", [P, 1])
        ones = sb("ones", [P, P], BF16)
        upto = sb("upto", [P, P], BF16)
        after = sb("after", [P, P], BF16)
        ones_f = sb("ones_f", [P, P])
        upto_f = sb("upto_f", [P, P])
        bases = sb("bases", [P, GROUP, P])
        hot = sb("hot", [P, R, SORT_GROUPS, GROUP, P], BF16)
        count_row = sb("count_row", [P, P])
        count_col = sb("count_col", [P, 1])
        exceeded = sb("exceeded", [P, block_chunks])
        chunks = sb("chunks", [P, 1])
        chunks_b = sb("chunks_b", [P, P])
        ended = sb("ended", [P, 1])
        passed = sb("passed", [P, max_chunks])
        total = sb("total", [1, 1])
        pairs = sb("pairs", [1, max_chunks // 2])
        pairs_f = sb("pairs_f", [1, 1])
        own = sb("own", [P, 2, GROUP, P])
        rank = sb("rank", [P, R, SORT_TILES])
        place = sb("place", [P, R, SORT_TILES], I32)
        staged = sb("staged", [P, R, SORT_TILES, 2], I32)
        counts_ps = pb("counts_ps", [P, GROUP, P])
        ranks_ps = pb("ranks_ps", [P, GROUP, P])
        col_ps = pb("col_ps", [P, 512])
        ended_ps = pb("ended_ps", [P, 512])
        block_ps = pb("block_ps", [P, 512])
        total_ps = pb("total_ps", [P, 512])

        loaded = sem("loaded")
        pool_consts = sem("pool_consts")
        fill_ready = sem("fill_ready")
        filled = sem("filled")
        consts = sem("consts")
        hot_counted = sem("hot_counted")
        hot_to_count = sem("hot_to_count")
        counts_read = sem("counts_read")
        products = sem("products")
        hot_ready = sem("hot_ready")
        ranks_in_psum = sem("ranks_in_psum")
        ranks_read = sem("ranks_read")
        hot_passed = sem("hot_passed")
        places_ready = sem("places_ready")
        scatter_begun = sem("scatter_begun")
        scattered = [queue_sem(nc, f"gat_scattered{s}") for s in range(R)]

        with nc.Block() as block:
            @block.sync
            def _(sp):
                sp.dma_start(dst[:, :], edge_index[1].rearrange("(p t) -> p t", p=P)).then_inc(loaded, 16)
                sp.dma_start(src[:, :], edge_index[0].rearrange("(p t) -> p t", p=P)).then_inc(loaded, 16)
                sp.wait_ge(fill_ready, 2)
                parts = sorted_edges.rearrange("(s p k) c -> s p k c", s=FILLS, p=P)
                for s in range(FILLS):
                    sp.dma_start(parts[s], fill[:, :, :]).then_inc(filled, 16)

            @block.gpsimd
            def _(pool):
                nc.gpsimd.iota(iota_i[:, :], pattern=[[1, 512]], base=0, channel_multiplier=0).then_inc(pool_consts, 1)
                nc.gpsimd.iota(row_i[:, :], pattern=[[0, 1]], base=0, channel_multiplier=1).then_inc(pool_consts, 1)
                nc.gpsimd.memset(fill[:, :, 0], 0).then_inc(fill_ready, 1)
                nc.gpsimd.memset(fill[:, :, 1], P).then_inc(fill_ready, 1)
                last_slot = pool.to_reg(slots - 1)

                def scatter(q, u):
                    pool.wait_ge(filled, 16 * FILLS)
                    before(pool, places_ready, q, u, 0)
                    pool.sem_inc(scatter_begun, 1)
                    for j in range(SORT_TILES):
                        nc.gpsimd.indirect_dma_start(
                            out=sorted_edges, out_offset=bass.IndirectOffsetOnAxis(ap=place[:, u, j:j + 1], axis=0),
                            in_=staged[:, u, j, :], in_offset=None, bounds_check=last_slot,
                            oob_is_err=False).then_inc(scattered[u], 16)

                sweep(pool, units, [(0, scatter)])
                for s in range(R):
                    pool.wait_ge(scattered[s], 16 * SORT_TILES * (units // R))

            @block.tensor
            def _(pe):
                pe.wait_ge(consts, 1)

                def count(q, u):
                    before(pe, hot_to_count, q, u, 0)
                    for g in range(SORT_GROUPS):
                        first = isinstance(q, int) and q * R + u + g == 0
                        last = nc.tensor.matmul(counts_ps[:, :, :], ones[:, :], hot[:, u, g], start=first, stop=False,
                                                skip_group_check=True)
                    last.then_inc(hot_counted, 1)

                sweep(pe, units, [(0, count)])
                pe.wait_ge(counts_read, 1)
                nc.tensor.matmul(col_ps[:, 0:1], count_row[0:1, :], ones_f[0:1, 0:1], start=True,
                                 stop=True).then_inc(products, 1)
                pe.wait_ge(counts_read, 2)
                nc.tensor.matmul(ranks_ps[:, :, :], chunks_b[:, :], bases[:, :, :], start=True, stop=False,
                                 skip_group_check=True)
                nc.tensor.matmul(total_ps[0:1, 0:1], chunks[:, 0:1], ones_f[:, 0:1], start=True, stop=True)
                nc.tensor.matmul(ended_ps[:, 0:1], upto_f[:, :], chunks[:, 0:1], start=True,
                                 stop=True).then_inc(products, 1)
                pe.wait_ge(counts_read, 3)
                nc.tensor.matmul(block_ps[0:1, 0:max_chunks], ones_f[:, 0:1], passed[:, :], start=True,
                                 stop=True).then_inc(products, 1)

                def rank_group(q, u):
                    before(pe, hot_ready, q, u, 0)
                    for g in range(SORT_GROUPS):
                        add = lambda to, w, of: nc.tensor.matmul(ranks_ps[:, to], w[:, :], hot[:, u, g, of],
                                                                 start=False, stop=False, skip_group_check=True)
                        for s in range(1, GROUP):
                            add(slice(s, GROUP), ones, slice(0, GROUP - s))
                        add(slice(0, GROUP), upto, slice(0, GROUP)).then_inc(ranks_in_psum, 1)
                        group_wait(pe, ranks_read, q, u, g)
                        for s in range(1, GROUP):
                            add(slice(0, GROUP - s), ones, slice(s, GROUP))
                        last = add(slice(0, GROUP), after, slice(0, GROUP))
                    last.then_inc(hot_passed, 1)

                sweep(pe, units, [(0, rank_group)])

            @block.vector
            def _(dve):
                dve.wait_ge(pool_consts, 2)
                setup = Chain(nc, ctx, dve, "sort_setup", 40)
                setup.unit(0)
                link = setup.link
                nc.vector.memset(ones[:, :], 1.0)
                nc.vector.memset(ones_f[:, :], 1.0)
                nc.vector.tensor_copy(row_f[:, :], row_i[:, :])
                link(nc.vector.tensor_copy(iota_f[:, :], iota_i[:, :]))
                nc.vector.tensor_scalar(upto[:, :], iota_f[:, 0:P], row_f[:, 0:1], None, ALU.is_ge)
                nc.vector.tensor_scalar(upto_f[:, :], iota_f[:, 0:P], row_f[:, 0:1], None, ALU.is_ge)
                nc.vector.tensor_scalar(after[:, :], iota_f[:, 0:P], row_f[:, 0:1], None, ALU.is_lt)
                for k in range(GROUP):
                    last = nc.vector.tensor_scalar(bases[:, k], iota_f[:, 0:P], row_f[:, 0:1], float(CHUNK),
                                                   ALU.is_gt, ALU.mult)
                last.then_inc(consts, 1)
                dve.wait_ge(loaded, 32)
                nc.vector.tensor_scalar(payload[:, :, 1], dst[:, :], P - 1, None, ALU.bitwise_and)
                link(nc.vector.tensor_scalar(work_i[:, :], dst[:, :], P.bit_length() - 1, None, ALU.arith_shift_right))
                link(nc.vector.tensor_copy(blk[:, :], work_i[:, :]))
                link(nc.vector.tensor_scalar(shift[:, :], blk[:, :], 0.0, INVALID, ALU.is_lt, ALU.mult))
                link(nc.vector.tensor_scalar(src_f[:, :], blk[:, :], float(P), INVALID, ALU.is_ge, ALU.mult))
                link(nc.vector.scalar_tensor_tensor(out=shift[:, :], in0=shift[:, :], scalar=-1.0, in1=src_f[:, :],
                                                    op0=ALU.add, op1=ALU.add))
                link(nc.vector.tensor_copy(src_f[:, :], src[:, :]))
                wrap = payload[:, :, 0].bitcast(F32)
                link(nc.vector.tensor_scalar(wrap, src_f[:, :], 0.0, float(n_nodes), ALU.is_lt, ALU.mult))
                link(nc.vector.tensor_tensor(src_f[:, :], src_f[:, :], wrap, ALU.add))
                link(nc.vector.tensor_scalar(payload[:, :, 0], src_f[:, :], float(n_nodes - 1), 0.0, ALU.min, ALU.max))

                def heat(q, u, signal):
                    for g in range(SORT_GROUPS):
                        at = (q * R + u) * SORT_TILES + g * GROUP
                        col = blk[:, bass.ds(at, GROUP)] if not isinstance(at, int) else blk[:, at:at + GROUP]
                        last = nc.vector.tensor_tensor(
                            hot[:, u, g], iota_f[:, 0:P].unsqueeze(1).to_broadcast([P, GROUP, P]),
                            col.unsqueeze(2).to_broadcast([P, GROUP, P]), ALU.is_equal)
                    last.then_inc(signal, 1)

                def heat_to_count(q, u):
                    before(dve, hot_counted, q, u, R)
                    heat(q, u, hot_to_count)

                sweep(dve, units, [(0, heat_to_count)])
                dve.wait_ge(hot_counted, units)
                link(nc.vector.tensor_reduce(count_row[:, :], counts_ps[:, :, :].rearrange("p k b -> p b k"),
                                             AX_X, ALU.add))
                nc.vector.tensor_scalar(exceeded[:, :], iota_f[:, 0:block_chunks], float(CHUNK), None,
                                        ALU.mult).then_inc(counts_read, 1)
                dve.wait_ge(products, 1)
                link(nc.vector.tensor_copy(count_col[:, :], col_ps[:, 0:1]))
                link(nc.vector.tensor_scalar(exceeded[:, :], exceeded[:, :], count_col[:, 0:1], None, ALU.is_lt))
                link(nc.vector.tensor_reduce(chunks[:, :], exceeded[:, :], AX_X, ALU.add))
                nc.vector.tensor_scalar(chunks_b[:, :], ones_f[:, :], chunks[:, 0:1], None,
                                        ALU.mult).then_inc(counts_read, 1)
                dve.wait_ge(products, 2)
                nc.vector.tensor_copy(total[:, :], total_ps[0:1, 0:1])
                link(nc.vector.tensor_copy(ended[:, :], ended_ps[:, 0:1]))
                nc.vector.tensor_scalar(passed[:, :], iota_f[:, 0:max_chunks], ended[:, 0:1], None,
                                        ALU.is_ge).then_inc(counts_read, 1)
                link(nc.vector.tensor_scalar(pairs[:, :], iota_f[0:1, 0:max_chunks // 2], 2.0, total[0:1, 0:1],
                                             ALU.mult, ALU.is_lt))
                link(nc.vector.tensor_reduce(pairs_f[:, :], pairs[:, :], AX_X, ALU.add))
                link(nc.vector.tensor_scalar(pair_count[:, :], pairs_f[:, :], 1.0, None, ALU.max))
                dve.wait_ge(products, 3)
                link(nc.vector.tensor_scalar(chunk_block[:, :], block_ps[0:1, 0:max_chunks], float(P - 1), None,
                                             ALU.min))

                place_steps = Chain(nc, ctx, dve, "sort_place_steps", SORT_GROUPS + 2)

                def heat_to_rank(q, u):
                    before(dve, hot_passed, q, u, R)
                    heat(q, u, hot_ready)

                def take_places(q, u):
                    place_steps.unit(q * R + u)
                    for g in range(SORT_GROUPS):
                        group_wait(dve, ranks_in_psum, q, u, g)
                        last = nc.vector.tensor_tensor(own[:, g % 2], ranks_ps[:, :, :], hot[:, u, g], ALU.mult)
                        last.then_inc(ranks_read, 1)
                        group_wait(dve, ranks_read, q, u, g)
                        place_steps.link(nc.vector.tensor_reduce(rank[:, u, g * GROUP:(g + 1) * GROUP], own[:, g % 2],
                                                                 AX_X, ALU.add))
                    at = (q * R + u) * SORT_TILES
                    cols = slice(at, at + SORT_TILES) if isinstance(at, int) else bass.ds(at, SORT_TILES)
                    slot_ready_n(dve, scattered, q, u, 1, SORT_TILES)
                    nc.vector.tensor_copy(staged[:, u], payload[:, cols, :])
                    place_steps.link(nc.vector.tensor_tensor(rank[:, u], rank[:, u], shift[:, cols], ALU.add))
                    place_steps.link(nc.vector.tensor_copy(place[:, u], rank[:, u]))
                    place_steps.end()
                    nc.vector.tensor_copy(staged[:, u, :, 1], payload[:, cols, 1]).then_inc(places_ready, 1)

                sweep(dve, units, [(0, heat_to_rank), (1, take_places)])


def group_wait(eng, s, q, u, g):
    eng.wait_ge(s, (q * R + u) * SORT_GROUPS + (g + 1))


def slot_ready_n(eng, sems, q, u, back, n):
    if isinstance(q, int):
        if q + 1 - back > 0:
            eng.wait_ge(sems[u], 16 * n * (q + 1 - back))
    else:
        eng.wait_ge(sems[u], (q + (1 - back)) * (16 * n))


STATE = HEADS + FEATS


def attention_stage(nc, ident_b, node_rows, table, sorted_edges, chunk_block, pair_count, agg):
    slots = sorted_edges.shape[0]
    max_chunks = chunk_block.shape[1]
    blocks = node_rows.shape[1]
    HL = HEADS * LEVELS
    SPLIT = 3
    TURN = 8
    NEAR = 2 * HEADS
    with ExitStack() as ctx:
        sb = lambda n, shape, dt=F32: ctx.enter_context(nc.sbuf_tensor(f"att_{n}", shape, dt))
        pb = lambda n, shape, dt=F32: ctx.enter_context(nc.psum_tensor(f"att_{n}", shape, dt))
        sem = lambda n: ctx.enter_context(nc.semaphore(f"att_{n}"))
        iota_i = sb("iota_i", [P, P], I32)
        iota_f = sb("iota_f", [P, P])
        top_part = sb("top_part", [P, HEADS])
        top = sb("top", [P, HEADS])
        lowest = sb("lowest", [P, HEADS])
        levels = sb("levels", [P, HEADS, LEVELS])
        state = sb("state", [P, blocks, STATE])
        edges = sb("edges", [P, 2, TILES, 2], I32)
        rows = sb("rows", [P, 2, TILES, ROW])
        near_f = sb("near_f", [P, TILES])
        hot = sb("hot", [P, 2, TILES, P], BF16)
        hotT = sb("hotT", [P, 2, TILES, P], BF16)
        above = sb("above", [P, 2, TILES, HL], BF16)
        reached = sb("reached", [P, HEADS, LEVELS])
        n_levels = sb("n_levels", [P, HEADS])
        old = sb("old", [P, STATE])
        a_dst = sb("a_dst", [P, HEADS])
        maxima = sb("maxima", [P, 2, HEADS])
        logits = sb("logits", [P, 2, HEADS])
        shifts = sb("shifts", [P, 2, HEADS])
        growth = sb("growth", [P, HEADS])
        decay = sb("decay", [P, HEADS])
        near = sb("near", [P, NEAR])
        near_rest = sb("near_rest", [P, 2, NEAR])
        near_parts = sb("near_parts", [P, 2, NEAR, SPLIT], BF16)
        got = sb("got", [P, TILES, NEAR])
        s_edge = sb("s_edge", [P, TILES, HEADS])
        l_edge = sb("l_edge", [P, TILES, HEADS])
        w_arg = sb("w_arg", [P, TILES, HEADS])
        weight = sb("weight", [P, TILES, HEADS])
        msg = sb("msg", [P, TILES, FEATS])
        msg_rest = sb("msg_rest", [P, 2, TILES, FEATS])
        msg_parts = sb("msg_parts", [P, 2, TILES, SPLIT, FEATS], BF16)
        added = sb("added", [P, FEATS])
        new = sb("new", [P, STATE])
        decayed = sb("decayed", [P, FEATS])
        denom = sb("denom", [P, blocks, HEADS])
        hotT_ps = pb("hotT_ps", [P, 2, TURN, P], BF16)
        levels_ps = pb("levels_ps", [P, 2, 512])
        near_ps = pb("near_ps", [P, 2, 512])
        sums_ps = pb("sums_ps", [P, 2, 512])

        iota_done = sem("iota_done")
        top_parts = sem("top_parts")
        top_done = sem("top_done")
        edges_free = sem("edges_free")
        edges_loaded = [sem(f"edges_loaded{s}") for s in range(2)]
        gather_begun = sem("gather_begun")
        rows_free = sem("rows_free")
        rows_gathered = [queue_sem(nc, f"gat_rows_gathered{s}") for s in range(2)]
        hot_ready = sem("hot_ready")
        hotT_in_psum = sem("hotT_in_psum")
        hotT_free = sem("hotT_free")
        hotT_ready = sem("hotT_ready")
        above_ready = sem("above_ready")
        levels_in_psum = sem("levels_in_psum")
        growth_ready = sem("growth_ready")
        decay_ready = sem("decay_ready")
        near_ready = sem("near_ready")
        near_in_psum = sem("near_in_psum")
        w_arg_ready = sem("w_arg_ready")
        weight_ready = sem("weight_ready")
        part_ready = sem("part_ready")
        part_copied = sem("part_copied")
        msg_ready = sem("msg_ready")
        sums_in_psum = sem("sums_in_psum")

        turns = [(t, min(t + TURN, TILES)) for t in range(0, TILES, TURN)]
        chunk_rows = sorted_edges.rearrange("(c p t) k -> c p t k", p=P, t=TILES)

        def wait_unit(eng, s, q, u, each=1):
            eng.wait_ge(s, q * (2 * each) + (u + 1) * each)

        def wait_slot(eng, sems, q, u, n=1):
            eng.wait_ge(sems[u], q * (16 * n) + 16 * n)

        def n_pairs(eng):
            return eng.value_load(pair_count[0:1, 0:1], min_val=1, max_val=max_chunks // 2)

        with nc.Block() as block:
            @block.sync
            def _(sp):
                with sp.Fori(0, n_pairs(sp)) as q:
                    for u in range(2):
                        wait_unit(sp, edges_free, q, u)
                        sp.dma_start(edges[:, u], chunk_rows[q * 2 + u]).then_inc(edges_loaded[u], 16)

            @block.gpsimd
            def _(pool):
                nc.gpsimd.iota(iota_i[:, :], pattern=[[1, P]], base=0, channel_multiplier=0).then_inc(iota_done, 1)
                pool.wait_ge(top_parts, 1)
                nc.gpsimd.partition_all_reduce(top[:, :], top_part[:, :], P, RMAX).then_inc(top_done, 1)
                with pool.Fori(0, n_pairs(pool)) as q:
                    for u in range(2):
                        wait_slot(pool, edges_loaded, q, u)
                        wait_unit(pool, rows_free, q, u)
                        pool.sem_inc(gather_begun, 1)
                        for t in range(TILES):
                            nc.gpsimd.indirect_dma_start(
                                out=rows[:, u, t, :], out_offset=None, in_=table,
                                in_offset=bass.IndirectOffsetOnAxis(ap=edges[:, u, t, 0:1], axis=0)
                            ).then_inc(rows_gathered[u], 16)

            @block.tensor
            def _(pe):
                with pe.Fori(0, n_pairs(pe)) as q:
                    for u in range(2):
                        wait_unit(pe, hot_ready, q, u)
                        for k, (a, b) in enumerate(turns):
                            pe.wait_ge(hotT_free, (q * 2 + u) * len(turns) + (k + 1))
                            bank = (u * len(turns) + k) % 2
                            for t in range(a, b):
                                last = nc.tensor.transpose(hotT_ps[:, bank, t - a], hot[:, u, t], ident_b[:, :])
                            last.then_inc(hotT_in_psum, 1)
                        wait_unit(pe, above_ready, q, u)
                        for t in range(TILES):
                            last = nc.tensor.matmul(levels_ps[:, u, 0:HL], hot[:, u, t], above[:, u, t],
                                                    start=(t == 0), stop=(t == TILES - 1))
                        last.then_inc(levels_in_psum, 1)
                        wait_unit(pe, near_ready, q, u)
                        wait_unit(pe, hotT_ready, q, u, len(turns))
                        for t in range(TILES):
                            last = nc.tensor.matmul(near_ps[:, u, t * NEAR * SPLIT:(t + 1) * NEAR * SPLIT],
                                                    hotT[:, u, t], near_parts[:, u], start=True, stop=True)
                        last.then_inc(near_in_psum, 1)
                        wait_unit(pe, msg_ready, q, u)
                        for t in range(TILES):
                            last = nc.tensor.matmul(sums_ps[:, u, 0:SPLIT * FEATS], hot[:, u, t], msg_parts[:, u, t],
                                                    start=(t == 0), stop=(t == TILES - 1))
                        last.then_inc(sums_in_psum, 1)

            @block.scalar
            def _(act):
                act.sem_inc(hotT_free, 2)
                with act.Fori(0, n_pairs(act)) as q:
                    for u in range(2):
                        for k, (a, b) in enumerate(turns):
                            act.wait_ge(hotT_in_psum, (q * 2 + u) * len(turns) + (k + 1))
                            bank = (u * len(turns) + k) % 2
                            nc.scalar.copy(hotT[:, u, a:b], hotT_ps[:, bank, 0:b - a]).then_inc(hotT_ready, 1)
                            act.wait_ge(hotT_ready, (q * 2 + u) * len(turns) + (k + 1))
                            act.sem_inc(hotT_free, 1)
                        wait_unit(act, growth_ready, q, u)
                        nc.scalar.activation(decay[:, :], growth[:, :], ACT.Exp).then_inc(decay_ready, 1)
                        wait_unit(act, w_arg_ready, q, u)
                        nc.scalar.activation(weight[:, :, :], w_arg[:, :, :], ACT.Exp).then_inc(weight_ready, 1)
                        for k in range(2):
                            act.wait_ge(part_ready, (q * 2 + u) * 2 + (k + 1))
                            source = msg[:, :, :] if k == 0 else msg_rest[:, 0]
                            nc.scalar.copy(msg_parts[:, u, :, k], source).then_inc(part_copied, 1)

            @block.vector
            def _(dve):
                setup = Chain(nc, ctx, dve, "att_setup", 40)
                setup.unit(0)
                link = setup.link
                nc.vector.tensor_reduce(top_part[:, :], node_rows[:, :, FEATS:ROW].rearrange("p g h -> p h g"),
                                        AX_X, ALU.max).then_inc(top_parts, 1)
                dve.wait_ge(iota_done, 1)
                link(nc.vector.tensor_copy(iota_f[:, :], iota_i[:, :]))
                link(nc.vector.tensor_scalar(levels[:, :, :],
                                             iota_f[:, 0:LEVELS].unsqueeze(1).to_broadcast([P, HEADS, LEVELS]),
                                             1.0, -LEVEL_STEP, ALU.add, ALU.mult))
                dve.wait_ge(top_done, 1)
                link(nc.vector.tensor_tensor(levels[:, :, :], levels[:, :, :],
                                             top[:, :].unsqueeze(2).to_broadcast([P, HEADS, LEVELS]), ALU.add))
                nc.vector.tensor_copy(state[:, :, 0:HEADS], node_rows[:, :, FEATS:ROW])
                nc.vector.tensor_copy(state[:, :, HEADS:STATE], node_rows[:, :, 0:FEATS])
                link(nc.vector.tensor_scalar(lowest[:, :], top[:, :], -LEVEL_STEP * LEVELS, None, ALU.add))
                dve.sem_inc(edges_free, 2)
                dve.sem_inc(rows_free, 2)
                steps = Chain(nc, ctx, dve, "att_steps", 21)
                pairs = n_pairs(dve)

                def targets(c, q, u):
                    wait_slot(dve, rows_gathered, q, u, TILES)
                    steps.link(nc.vector.tensor_copy(near_f[:, :], edges[:, u, :, 1]))
                    nc.vector.tensor_tensor(hot[:, u], iota_f[:, :].unsqueeze(1).to_broadcast([P, TILES, P]),
                                            near_f[:, :].unsqueeze(2).to_broadcast([P, TILES, P]),
                                            ALU.is_equal).then_inc(hot_ready, 1)
                    dve.sem_inc(edges_free, 1)
                    nc.vector.tensor_tensor(
                        above[:, u].rearrange("p t (h l) -> p t h l", h=HEADS),
                        rows[:, u, :, FEATS:ROW].unsqueeze(3).to_broadcast([P, TILES, HEADS, LEVELS]),
                        levels[:, :, :].unsqueeze(1).to_broadcast([P, TILES, HEADS, LEVELS]),
                        ALU.is_ge).then_inc(above_ready, 1)

                def maximum(c, q, u, blk):
                    nc.vector.tensor_scalar(old[:, :], state[:, blk, :], 1.0, None, ALU.mult)
                    steps.link(nc.vector.tensor_scalar(a_dst[:, :], node_rows[:, blk, ROW:NODE_ROW], 1.0, None,
                                                       ALU.mult))
                    nc.vector.tensor_copy(maxima[:, 0], old[:, 0:HEADS])
                    nc.vector.tensor_copy(near[:, 0:HEADS], a_dst[:, :])
                    wait_unit(dve, levels_in_psum, q, u)
                    steps.link(nc.vector.tensor_scalar(reached[:, :, :],
                                                       levels_ps[:, u, 0:HL].rearrange("p (h l) -> p h l", h=HEADS),
                                                       0.0, None, ALU.is_gt))
                    steps.link(nc.vector.tensor_reduce(n_levels[:, :], reached[:, :, :], AX_X, ALU.add))
                    steps.link(nc.vector.scalar_tensor_tensor(out=maxima[:, 1], in0=n_levels[:, :], scalar=LEVEL_STEP,
                                                              in1=lowest[:, :], op0=ALU.mult, op1=ALU.add))
                    steps.link(nc.vector.tensor_tensor(maxima[:, 1], maxima[:, 1], old[:, 0:HEADS], ALU.max))
                    steps.link(nc.vector.tensor_tensor(logits[:, :, :], maxima[:, :, :],
                                                       a_dst[:, :].unsqueeze(1).to_broadcast([P, 2, HEADS]), ALU.add))
                    steps.link(nc.vector.scalar_tensor_tensor(out=shifts[:, :, :], in0=logits[:, :, :],
                                                              scalar=NEG_SLOPE, in1=logits[:, :, :],
                                                              op0=ALU.mult, op1=ALU.max))
                    nc.vector.tensor_copy(near[:, HEADS:NEAR], shifts[:, 1])
                    steps.link(nc.vector.tensor_tensor(growth[:, :], shifts[:, 0], shifts[:, 1], ALU.subtract))
                    dve.sem_inc(growth_ready, 1)
                    steps.link(nc.vector.tensor_copy(near_parts[:, u, :, 0], near[:, :]))
                    steps.link(nc.vector.tensor_tensor(near_rest[:, 0], near[:, :], near_parts[:, u, :, 0], ALU.subtract))
                    steps.link(nc.vector.tensor_copy(near_parts[:, u, :, 1], near_rest[:, 0]))
                    nc.vector.tensor_tensor(near_parts[:, u, :, 2], near_rest[:, 0], near_parts[:, u, :, 1],
                                            ALU.subtract).then_inc(near_ready, 1)

                def weigh(c, q, u):
                    wait_unit(dve, near_in_psum, q, u)
                    steps.link(nc.vector.tensor_reduce(
                        got[:, :, :], near_ps[:, u, 0:TILES * NEAR * SPLIT].rearrange("p (t k s) -> p t k s", t=TILES, s=SPLIT),
                        AX_X, ALU.add))
                    steps.link(nc.vector.tensor_tensor(s_edge[:, :, :], rows[:, u, :, FEATS:ROW], got[:, :, 0:HEADS], ALU.add))
                    steps.link(nc.vector.scalar_tensor_tensor(out=l_edge[:, :, :], in0=s_edge[:, :, :], scalar=NEG_SLOPE,
                                                              in1=s_edge[:, :, :], op0=ALU.mult, op1=ALU.max))
                    nc.vector.tensor_tensor(w_arg[:, :, :], l_edge[:, :, :], got[:, :, HEADS:NEAR],
                                            ALU.subtract).then_inc(w_arg_ready, 1)
                    wait_unit(dve, weight_ready, q, u)
                    steps.link(nc.vector.tensor_tensor(
                        msg[:, :, :].rearrange("p t (h c) -> p t h c", h=HEADS),
                        rows[:, u, :, 0:FEATS].rearrange("p t (h c) -> p t h c", h=HEADS),
                        weight[:, :, :].unsqueeze(3).to_broadcast([P, TILES, HEADS, EXPERTS + 1]), ALU.mult))
                    dve.sem_inc(rows_free, 1)
                    dve.sem_inc(part_ready, 1)
                    dve.wait_ge(part_copied, (q * 2 + u) * 2 + 1)
                    steps.link(nc.vector.tensor_tensor(msg_rest[:, 0], msg[:, :, :], msg_parts[:, u, :, 0], ALU.subtract))
                    dve.sem_inc(part_ready, 1)
                    dve.wait_ge(part_copied, (q * 2 + u) * 2 + 2)
                    nc.vector.tensor_tensor(msg_parts[:, u, :, 2], msg_rest[:, 0], msg_parts[:, u, :, 1],
                                            ALU.subtract).then_inc(msg_ready, 1)

                def merge(c, q, u, blk):
                    wait_unit(dve, decay_ready, q, u)
                    steps.link(nc.vector.tensor_tensor(
                        decayed[:, :].rearrange("p (h c) -> p h c", h=HEADS),
                        old[:, HEADS:STATE].rearrange("p (h c) -> p h c", h=HEADS),
                        decay[:, :].unsqueeze(2).to_broadcast([P, HEADS, EXPERTS + 1]), ALU.mult))
                    nc.vector.tensor_copy(new[:, 0:HEADS], maxima[:, 1])
                    wait_unit(dve, sums_in_psum, q, u)
                    steps.link(nc.vector.tensor_reduce(
                        added[:, :], sums_ps[:, u, 0:SPLIT * FEATS].rearrange("p (s f) -> p f s", s=SPLIT), AX_X, ALU.add))
                    steps.link(nc.vector.tensor_tensor(new[:, HEADS:STATE], decayed[:, :], added[:, :], ALU.add))
                    steps.link(nc.vector.tensor_scalar(state[:, blk, :], new[:, :], 1.0, None, ALU.mult))

                with dve.Fori(0, pairs) as q:
                    for u in range(2):
                        c = q * 2 + u
                        steps.unit(c)
                        blk = dve.value_load(chunk_block[0:1, bass.ds(c, 1)], min_val=0, max_val=blocks - 1)
                        targets(c, q, u)
                        maximum(c, q, u, blk)
                        weigh(c, q, u)
                        merge(c, q, u, blk)
                        steps.end()
                sums = state[:, :, HEADS:STATE].rearrange("p g (h c) -> p g h c", h=HEADS)
                link(nc.vector.reciprocal(denom[:, :, :], sums[:, :, :, EXPERTS]))
                link(nc.vector.tensor_tensor(agg.rearrange("p g (h c) -> p g h c", h=HEADS), sums[:, :, :, 0:EXPERTS],
                                             denom[:, :, :].unsqueeze(3).to_broadcast([P, blocks, HEADS, EXPERTS]),
                                             ALU.mult))




TOP_K = 2


def gate_stage(nc, agg, b_gat, ln_gamma, ln_beta, gates):
    graphs = agg.shape[1]
    with ExitStack() as ctx:
        sb = lambda n, shape, dt=F32: ctx.enter_context(nc.sbuf_tensor(f"gate_{n}", shape, dt))
        sem = lambda n: ctx.enter_context(nc.semaphore(f"gate_{n}"))
        rows = sb("rows", [P, 3, HE])
        a = sb("a", [P, graphs, HE])
        b = sb("b", [P, graphs, HE])
        mean = sb("mean", [P, graphs])
        var = sb("var", [P, graphs])
        root = sb("root", [P, graphs])
        rstd = sb("rstd", [P, graphs])
        scores = sb("scores", [P, graphs, EXPERTS])
        best = sb("best", [P, graphs])
        gap = sb("gap", [P, graphs, EXPERTS])
        e = sb("e", [P, graphs, EXPERTS])
        masks = sb("masks", [P, 2, EXPERTS, EXPERTS])
        beats = sb("beats", [P, graphs, EXPERTS, EXPERTS])
        ties = sb("ties", [P, graphs, EXPERTS, EXPERTS])
        ahead = sb("ahead", [P, graphs, EXPERTS])
        chosen = sb("chosen", [P, graphs, EXPERTS])
        loaded, asked, rooted, shifted, raised = (sem(n) for n in ("loaded", "asked", "rooted", "shifted", "raised"))
        wide = lambda ap: ap.unsqueeze(2).to_broadcast([P, graphs, HE])
        row = lambda k: rows[:, k:k + 1, :].to_broadcast([P, graphs, HE])

        with nc.Block() as block:
            @block.sync
            def _(sp):
                for k, source in enumerate((b_gat, ln_gamma, ln_beta)):
                    sp.dma_start(rows[:, k], source.partition_broadcast(P)).then_inc(loaded, 16)

            @block.scalar
            def _(act):
                act.wait_ge(asked, 1)
                nc.scalar.activation(root[:, :], var[:, :], ACT.Sqrt).then_inc(rooted, 1)
                act.wait_ge(shifted, 1)
                nc.scalar.activation(e[:, :, :], gap[:, :, :], ACT.Exp).then_inc(raised, 1)

            @block.vector
            def _(dve):
                steps = Chain(nc, ctx, dve, "gate_steps", 40)
                steps.unit(0)
                link = steps.link
                tt = nc.vector.tensor_tensor
                link(nc.vector.memset(masks[:, :, :, :], 0.0))
                for k in range(1, EXPERTS):
                    nc.vector.memset(masks[:, 0, k, 0:k], 1.0)
                    nc.vector.memset(masks[:, 1, k - 1, k:EXPERTS], 1.0)
                dve.wait_ge(loaded, 48)
                link(tt(a[:, :, :], agg, row(0), ALU.add))
                link(nc.vector.tensor_reduce(mean[:, :], a[:, :, :], AX_X, ALU.add))
                link(nc.vector.tensor_scalar(mean[:, :], mean[:, :], 1.0 / HE, None, ALU.mult))
                link(tt(a[:, :, :], a[:, :, :], wide(mean[:, :]), ALU.subtract))
                link(tt(b[:, :, :], a[:, :, :], a[:, :, :], ALU.mult))
                link(nc.vector.tensor_reduce(var[:, :], b[:, :, :], AX_X, ALU.add))
                nc.vector.tensor_scalar(var[:, :], var[:, :], 1.0 / HE, LN_EPS, ALU.mult, ALU.add).then_inc(asked, 1)
                dve.wait_ge(rooted, 1)
                link(nc.vector.reciprocal(rstd[:, :], root[:, :]))
                link(tt(a[:, :, :], a[:, :, :], wide(rstd[:, :]), ALU.mult))
                link(tt(a[:, :, :], a[:, :, :], row(1), ALU.mult))
                link(tt(a[:, :, :], a[:, :, :], row(2), ALU.add))
                link(nc.vector.tensor_reduce(scores[:, :, :], a[:, :, :].rearrange("p g (h e) -> p g e h", h=HEADS),
                                             AX_X, ALU.add))
                link(nc.vector.tensor_scalar(scores[:, :, :], scores[:, :, :], 1.0 / HEADS, None, ALU.mult))
                other = scores[:, :, :].unsqueeze(2).to_broadcast([P, graphs, EXPERTS, EXPERTS])
                this = scores[:, :, :].unsqueeze(3).to_broadcast([P, graphs, EXPERTS, EXPERTS])
                tt(beats[:, :, :, :], other, this, ALU.is_gt)
                link(tt(ties[:, :, :, :], other, this, ALU.is_ge))
                mask = lambda k: masks[:, k].rearrange("p e j -> p (e j)").unsqueeze(1).to_broadcast(
                    [P, graphs, EXPERTS * EXPERTS])
                flat = lambda ap: ap.rearrange("p g e j -> p g (e j)")
                tt(flat(beats[:, :, :, :]), flat(beats[:, :, :, :]), mask(1), ALU.mult)
                link(tt(flat(ties[:, :, :, :]), flat(ties[:, :, :, :]), mask(0), ALU.mult))
                link(tt(beats[:, :, :, :], beats[:, :, :, :], ties[:, :, :, :], ALU.add))
                link(nc.vector.tensor_reduce(ahead[:, :, :], beats[:, :, :, :], AX_X, ALU.add))
                nc.vector.tensor_scalar(chosen[:, :, :], ahead[:, :, :], TOP_K - 0.5, None, ALU.is_lt)
                link(nc.vector.tensor_reduce(best[:, :], scores[:, :, :], AX_X, ALU.max))
                tt(gap[:, :, :], scores[:, :, :], best[:, :].unsqueeze(2).to_broadcast([P, graphs, EXPERTS]),
                   ALU.subtract).then_inc(shifted, 1)
                dve.wait_ge(raised, 1)
                link(tt(e[:, :, :], e[:, :, :], chosen[:, :, :], ALU.mult))
                link(nc.vector.tensor_reduce(best[:, :], e[:, :, :], AX_X, ALU.add))
                link(nc.vector.reciprocal(rstd[:, :], best[:, :]))
                link(tt(gates, e[:, :, :], rstd[:, :].unsqueeze(2).to_broadcast([P, graphs, EXPERTS]), ALU.mult))


def expert_stage(nc, ident, x_in, x_out, gates, w1, b1, w2, b2):
    graphs = x_in.shape[0]
    units = graphs // QUAD
    HID = w1.shape[2] // P
    HB = EXPERTS * HID
    with ExitStack() as ctx:
        sb = lambda n, shape, dt=F32: ctx.enter_context(nc.sbuf_tensor(f"moe_{n}", shape, dt))
        pb = lambda n, shape, dt=F32: ctx.enter_context(nc.psum_tensor(f"moe_{n}", shape, dt))
        sem = lambda n: ctx.enter_context(nc.semaphore(f"moe_{n}"))
        w1_sb = sb("w1", [P, EXPERTS, HID * P])
        w2_sb = sb("w2", [P, EXPERTS, HID, P])
        b1_rows = sb("b1_rows", [HB, P])
        b1_sb = sb("b1", [P, HB])
        b2_sb = sb("b2", [QUAD * EXPERTS, QUAD, P])
        x_sb = sb("x", [P, R, QUAD, P])
        stats = sb("stats", [P, R, QUAD, 6])
        halves = sb("halves", [P, R, 3, QUAD])
        mean = sb("mean", [P, R, QUAD])
        var = sb("var", [P, R, QUAD])
        root_in = sb("root_in", [P, R, QUAD])
        root = sb("root", [P, R, QUAD])
        inv = sb("inv", [P, R, QUAD])
        gate = sb("gate", [P, R, QUAD, EXPERTS])
        gateT = sb("gateT", [QUAD * EXPERTS, R, P])
        xn = sb("xn", [P, R, QUAD, P])
        xnT = sb("xnT", [P, R, QUAD, P])
        hid = sb("hid", [P, 2, HB, QUAD * P])
        gated = sb("gated", [P, 2, EXPERTS, P])
        both = sb("both", [P, R, QUAD, P])
        xo = sb("xo", [P, R, QUAD, P])
        xnT_ps = pb("xnT_ps", [P, QUAD, P])
        gateT_ps = pb("gateT_ps", [P, 512])
        hid_ps = pb("hid_ps", [P, 2, QUAD * P])
        out_ps = pb("out_ps", [P, 2, EXPERTS, P])
        bias_ps = pb("bias_ps", [P, QUAD, P])

        weights_loaded = sem("weights_loaded")
        b2_zeroed = sem("b2_zeroed")
        b1_in_psum = sem("b1_in_psum")
        b1_ready = sem("b1_ready")
        x_loaded = [sem(f"x_loaded{s}") for s in range(R)]
        x_stored = [queue_sem(nc, f"moe_x_stored{s}") for s in range(R)]
        root_asked = sem("root_asked")
        root_ready = sem("root_ready")
        xn_ready = sem("xn_ready")
        xnT_in_psum = sem("xnT_in_psum")
        xnT_ready = sem("xnT_ready")
        hid_in_psum = sem("hid_in_psum")
        hid_ready = sem("hid_ready")
        out_in_psum = sem("out_in_psum")
        out_gated = sem("out_gated")
        bias_in_psum = sem("bias_in_psum")
        bias_added = sem("bias_added")
        x_done = sem("x_done")
        x_rows = x_in.rearrange("(g j) n f -> g n j f", j=QUAD)
        xo_rows = x_out.rearrange("(g j) n f -> g n j f", j=QUAD)

        def part_of(eng, s, q, u, k, n):
            eng.wait_ge(s, (q * R + u) * n + (k + 1))

        def part_before(eng, s, q, u, k, n, back):
            if isinstance(q, int):
                v = (q * R + u) * n + k + 1 - back
                if v > 0:
                    eng.wait_ge(s, v)
            else:
                eng.wait_ge(s, q * (R * n) + (u * n + k + 1 - back))

        with nc.Block() as block:
            @block.sync
            def _(sp):
                sp.dma_start(w1_sb[:, :, :], w1.rearrange("e f h -> f e h")).then_inc(weights_loaded, 16)
                sp.dma_start(w2_sb[:, :, :, :], w2.rearrange("e (c k) f -> k e c f", k=P)).then_inc(weights_loaded, 16)
                sp.dma_start(b1_rows[:, :], b1.rearrange("e (c k) -> (e c) k", k=P)).then_inc(weights_loaded, 16)
                sp.wait_ge(b2_zeroed, 1)
                for j in range(QUAD):
                    sp.dma_start(b2_sb[j * EXPERTS:(j + 1) * EXPERTS, j], b2).then_inc(weights_loaded, 16)

                def load(q, u):
                    before(sp, x_done, q, u, R)
                    sp.dma_start(x_sb[:, u], x_rows[q * R + u]).then_inc(x_loaded[u], 16)

                sweep(sp, units, [(0, load)])

            @block.gpsimd
            def _(pool):
                nc.gpsimd.memset(b2_sb[:, :, :], 0.0).then_inc(b2_zeroed, 1)

                def store(q, u):
                    before(pool, x_done, q, u, 0)
                    pool.dma_start(xo_rows[q * R + u], xo[:, u]).then_inc(x_stored[u], 16)

                sweep(pool, units, [(0, store)])
                for s in range(R):
                    pool.wait_ge(x_stored[s], 16 * (units // R))

            @block.tensor
            def _(pe):
                pe.wait_ge(weights_loaded, 16 * (3 + QUAD))
                nc.tensor.transpose(gateT_ps[:, 0:HB], b1_rows[:, :], ident[0:HB, 0:HB]).then_inc(b1_in_psum, 1)
                pe.wait_ge(b1_ready, 1)

                def transpose_xn(q, u):
                    before(pe, xn_ready, q, u, 0)
                    before(pe, xnT_ready, q, u, 1)
                    for j in range(QUAD):
                        nc.tensor.transpose(xnT_ps[:, j], xn[:, u, j], ident[:, :])
                    nc.tensor.transpose(gateT_ps[0:QUAD * EXPERTS, 0:P], gate[:, u].rearrange("p j e -> p (j e)"),
                                        ident[:, :]).then_inc(xnT_in_psum, 1)

                def hidden(q, u):
                    before(pe, xnT_ready, q, u, 0)
                    for k in range(HB):
                        part_before(pe, hid_ready, q, u, k, HB, 2)
                        nc.tensor.matmul(hid_ps[:, k % 2], w1_sb[:, k // HID, (k % HID) * P:(k % HID + 1) * P],
                                         xnT[:, u], start=True, stop=True).then_inc(hid_in_psum, 1)

                def output(q, u):
                    part_of(pe, hid_ready, q, u, HB - 1, HB)
                    for j in range(QUAD):
                        part_before(pe, out_gated, q, u, j, QUAD, 2)
                        for k in range(HB):
                            last = nc.tensor.matmul(out_ps[:, j % 2, k // HID], hid[:, u % 2, k, j * P:(j + 1) * P],
                                                    w2_sb[:, k // HID, k % HID], start=(k % HID == 0),
                                                    stop=(k % HID == HID - 1))
                        last.then_inc(out_in_psum, 1)
                    before(pe, bias_added, q, u, 1)
                    for j in range(QUAD):
                        last = nc.tensor.matmul(bias_ps[:, j], gateT[:, u], b2_sb[:, j], start=True, stop=True)
                    last.then_inc(bias_in_psum, 1)

                sweep(pe, units, [(0, transpose_xn), (1, hidden), (2, output)])

            @block.scalar
            def _(act):
                act.wait_ge(b1_in_psum, 1)
                nc.scalar.copy(b1_sb[:, :], gateT_ps[:, 0:HB]).then_inc(b1_ready, 1)
                act.wait_ge(b1_ready, 1)

                def take_root(q, u):
                    before(act, root_asked, q, u, 0)
                    before(act, xn_ready, q, u, R)
                    nc.scalar.activation(root[:, u], root_in[:, u], ACT.Sqrt).then_inc(root_ready, 1)

                def copy_xnT(q, u):
                    before(act, xnT_in_psum, q, u, 0)
                    part_before(act, hid_in_psum, q, u, HB - 1, HB, R * HB)
                    nc.scalar.copy(gateT[:, u], gateT_ps[0:QUAD * EXPERTS, 0:P])
                    nc.scalar.copy(xnT[:, u], xnT_ps[:, :]).then_inc(xnT_ready, 1)

                def bend(q, u):
                    part_before(act, out_in_psum, q, u, QUAD - 1, QUAD, 2 * QUAD)
                    for k in range(HB):
                        part_of(act, hid_in_psum, q, u, k, HB)
                        nc.scalar.activation(hid[:, u % 2, k], hid_ps[:, k % 2], ACT.Gelu,
                                             bias=b1_sb[:, k:k + 1]).then_inc(hid_ready, 1)

                sweep(act, units, [(0, take_root), (0, copy_xnT), (1, bend)])

            @block.vector
            def _(dve):
                stat_steps = Chain(nc, ctx, dve, "moe_stat_steps", 4)
                scale_steps = Chain(nc, ctx, dve, "moe_scale_steps", 1)
                gate_steps = Chain(nc, ctx, dve, "moe_gate_steps", QUAD + 1)

                def statistics(q, u):
                    stat_steps.unit(q * R + u)
                    slot_ready(dve, x_loaded, q, u)
                    for j in range(QUAD):
                        last = nc.vector.bn_stats(stats[:, u, j], x_sb[:, u, j])
                    stat_steps.link(last)
                    merge_statistics(nc, stat_steps, stats[:, u], mean[:, u], var[:, u], halves[:, u])
                    stat_steps.end()
                    nc.vector.tensor_scalar(root_in[:, u], var[:, u], LN_EPS, None, ALU.add).then_inc(root_asked, 1)

                def scale_x(q, u):
                    scale_steps.unit(q * R + u)
                    before(dve, root_ready, q, u, 0)
                    scale_steps.link(nc.vector.reciprocal(inv[:, u], root[:, u]))
                    before(dve, xnT_in_psum, q, u, R)
                    for j in range(QUAD):
                        nc.vector.tensor_scalar(xn[:, u, j], x_sb[:, u, j], mean[:, u, j:j + 1],
                                                inv[:, u, j:j + 1], ALU.subtract, ALU.mult)
                    at = (q * R + u) * QUAD
                    cols = slice(at, at + QUAD) if isinstance(at, int) else bass.ds(at, QUAD)
                    nc.vector.tensor_scalar(gate[:, u], gates[:, cols, :], 1.0, None, ALU.mult).then_inc(xn_ready, 1)

                def combine(q, u):
                    gate_steps.unit(q * R + u)
                    for j in range(QUAD):
                        part_of(dve, out_in_psum, q, u, j, QUAD)
                        gate_steps.link(nc.vector.tensor_tensor(
                            gated[:, j % 2], out_ps[:, j % 2], gate[:, u, j].unsqueeze(2).to_broadcast([P, EXPERTS, P]),
                            ALU.mult))
                        dve.sem_inc(out_gated, 1)
                        last = nc.vector.tensor_reduce(both[:, u, j], gated[:, j % 2].rearrange("p e f -> p f e"),
                                                       AX_X, ALU.add)
                    gate_steps.link(last)
                    before(dve, bias_in_psum, q, u, 0)
                    nc.vector.tensor_tensor(both[:, u], both[:, u], bias_ps[:, :, :], ALU.add).then_inc(bias_added, 1)
                    gate_steps.end()
                    before(dve, bias_added, q, u, 0)
                    slot_ready(dve, x_stored, q, u, 1)
                    nc.vector.tensor_tensor(xo[:, u], both[:, u], x_sb[:, u], ALU.add).then_inc(x_done, 1)

                sweep(dve, units, [(0, statistics), (0, scale_x), (2, combine)])




DECAY_MAX = 1e4
LOG_RATE_MAX = 69.0
SERIES = 7


def slice_stage(nc, ident, x_in, x_out, t):
    w = {k[len("L1_ffn_"):]: v for k, v in t.items() if k.startswith("L1_ffn_")}
    graphs = x_in.shape[0]
    units = graphs // QUAD
    H = w["hy_A_log"].shape[0]
    G = w["W_slice"].shape[0]
    D = w["W_fx"].shape[0]
    C = D // P
    NS = (w["hy_conv_w"].shape[0] - D) // 2
    K = w["hy_conv_w"].shape[1]
    PROJ = w["hy_in_w"].shape[0]
    DT = 2 * D + 2 * NS
    T = QUAD * G
    PAIRS = QUAD // 2
    assert G == 64 and NS == 64 and D // H == 64 and K == 3 and PROJ == DT + 2 * H
    HALF = 64
    x_stored = [queue_sem(nc, f"hy_x_stored{s}") for s in range(2)]
    with ExitStack() as ctx:
        sb = lambda n, shape, dt=F32: ctx.enter_context(nc.sbuf_tensor(f"hy_{n}", shape, dt))
        sem = lambda n: ctx.enter_context(nc.semaphore(f"hy_{n}"))
        bank = [ctx.enter_context(nc.psum_tensor(f"hy_bank{k}", [P, 512], F32)) for k in range(8)]

        w_fxT = sb("w_fxT", [P, D])
        w_logit = sb("w_logit", [P, D])
        b_fx = sb("b_fx", [P, D])
        b_logit = sb("b_logit", [P, D])
        in_wT = sb("in_wT", [P, C, PROJ])
        conv_x = sb("conv_x", [P, C, K])
        conv_bc = sb("conv_bc", [HALF, 2, K])
        convb_x = sb("convb_x", [P, C])
        convb_bc = sb("convb_bc", [HALF, 2])
        dt_bias = sb("dt_bias", [P, 2, H])
        rate = sb("rate", [P, 2, H])
        skip_w = sb("skip_w", [P, C, H])
        skip_b = sb("skip_b", [H, 1])
        spread = sb("spread", [H, C, 2, HALF])
        mix_w = sb("mix_w", [P, C, D])
        out_wT = sb("out_wT", [P, C, P])
        out_b = sb("out_b", [P, P])
        later = sb("later", [P, G])
        earlier = sb("earlier", [P, G])
        sum_later = sb("sum_later", [P, 2, G])
        sum_earlier = sb("sum_earlier", [P, 2, G])
        ones = sb("ones", [P, P])

        with ExitStack() as wctx:
            ws = lambda n, shape, dt=F32: wctx.enter_context(nc.sbuf_tensor(f"hyw_{n}", shape, dt))
            wsem = lambda n: wctx.enter_context(nc.semaphore(f"hyw_{n}"))
            fx_rows = ws("fx_rows", [P, C, P])
            x_rows_w = ws("x_rows", [P, C, P])
            slice_rows = ws("slice_rows", [G, 2, G])
            slice_wT = ws("slice_wT", [P, G])
            bx_rows = ws("bx_rows", [C, P])
            bx_cols = ws("bx_cols", [P, C])
            bx_wide = ws("bx_wide", [P, C, P])
            slice_b = ws("slice_b", [P, G])
            temp = ws("temp", [P, H])
            cold = ws("cold", [P, H])
            bias_sum = ws("bias_sum", [P, H, G])
            in_rows = ws("in_rows", [P, DT // P, D])
            dt_rows = ws("dt_rows", [2 * H, D])
            skip_rows = ws("skip_rows", [H, D])
            norm_rows = ws("norm_rows", [C, P])
            norm_cols = ws("norm_cols", [P, C])
            mix_rows = ws("mix_rows", [P, C, D])
            out_rows = ws("out_rows", [P, D])
            log_rate = ws("log_rate", [P, 2, H])
            iota_i = ws("iota_i", [P, G], I32)
            iota_f = ws("iota_f", [P, G])
            row_i = ws("row_i", [P, 1], I32)
            row_m = ws("row_m", [P, 1], I32)
            row_f = ws("row_f", [P, 1])
            loaded, pool_done, made, turned, kept = (wsem(n) for n in ("loaded", "pool_done", "made", "turned", "kept"))
            folded, w_steps = (wsem(n) for n in ("folded", "steps"))
            clear(nc, [loaded, pool_done, made, turned, kept, folded, w_steps])
            turns = [(norm_rows[:, :], norm_cols[:, :], None), (bx_rows[:, :], bx_cols[:, :], None),
                     (slice_rows[:, :, :].rearrange("g a p -> g (a p)"), slice_wT[:, :], None)]
            turns += [(fx_rows[:, c], w_fxT[:, c * P:(c + 1) * P], None) for c in range(C)]
            turns += [(in_rows[:, r, k * P:(k + 1) * P], in_wT[:, k, r * P:(r + 1) * P], None)
                      for r in range(DT // P) for k in range(C)]
            turns += [(dt_rows[:, k * P:(k + 1) * P], in_wT[:, k, DT:PROJ], None) for k in range(C)]
            turns += [(skip_rows[:, k * P:(k + 1) * P], skip_w[:, k], None) for k in range(C)]
            turns += [(mix_rows[:, r, k * P:(k + 1) * P], mix_w[:, k, r * P:(r + 1) * P], norm_cols[:, k:k + 1])
                      for r in range(C) for k in range(C)]
            turns += [(out_rows[:, k * P:(k + 1) * P], out_wT[:, k], None) for k in range(C)]
            BANKS = 6

            with nc.Block() as block:
                @block.sync
                def _(sp):
                    loads = [
                        (fx_rows[:, :, :], w["W_fx"].rearrange("(c k) f -> k c f", k=P)),
                        (x_rows_w[:, :, :], w["W_x"].rearrange("(c k) f -> k c f", k=P)),
                        (slice_rows[:, 0], w["W_slice"]), (slice_rows[:, 1], w["W_slice"]),
                        (bx_rows[:, :], w["b_x"].rearrange("(c k) -> c k", k=P)),
                        (slice_b[:, :], w["b_slice"].partition_broadcast(P)),
                        (temp[:, :], w["temperature"].rearrange("a h b c -> (a h b c)").partition_broadcast(P)),
                        (in_rows[:, :, :], w["hy_in_w"][0:DT].rearrange("(r k) c -> k r c", k=P)),
                        (dt_rows[:, :], w["hy_in_w"][DT:PROJ]),
                        (conv_x[:, :, :], w["hy_conv_w"][0:D].rearrange("(c k) w -> k c w", k=P)),
                        (conv_bc[:, :, :], w["hy_conv_w"][D:].rearrange("(c k) w -> k c w", k=HALF)),
                        (convb_x[:, :], w["hy_conv_b"][0:D].rearrange("(c k) -> k c", k=P)),
                        (convb_bc[:, :], w["hy_conv_b"][D:].rearrange("(c k) -> k c", k=HALF)),
                        (skip_b[:, :], w["hy_D"].rearrange("(h a) -> h a", a=1)),
                        (skip_rows[:, :], w["hy_fcD_w"]),
                        (norm_rows[:, :], w["hy_norm_w"].rearrange("(c k) -> c k", k=P)),
                        (mix_rows[:, :, :], w["hy_out_w"].rearrange("(r k) c -> k r c", k=P)),
                        (out_rows[:, :], w["out_w"]),
                        (out_b[:, :], w["out_b"].partition_broadcast(P)),
                        (b_fx[:, :], w["b_fx"].partition_broadcast(P)),
                    ]
                    for k in range(2):
                        loads.append((dt_bias[:, k], w["hy_dt_bias"].partition_broadcast(P)))
                        loads.append((log_rate[:, k], w["hy_A_log"].partition_broadcast(P)))
                    assert len(loads) == 24
                    with nc.allow_non_contiguous_dma(reason="a few hundred biases and taps, once"):
                        for to, source in loads:
                            sp.dma_start(to, source).then_inc(loaded, 16)

                @block.gpsimd
                def _(pool):
                    nc.gpsimd.iota(iota_i[:, :], pattern=[[1, G]], base=0, channel_multiplier=0).then_inc(pool_done, 1)
                    nc.gpsimd.iota(row_i[:, :], pattern=[[0, 1]], base=0, channel_multiplier=1).then_inc(pool_done, 1)
                    nc.gpsimd.memset(spread[:, :, :, :], 0.0).then_inc(pool_done, 1)
                    pool.wait_ge(pool_done, 3)
                    nc.gpsimd.affine_select(out=spread[:, :, :, :], in_=spread[:, :, :, :], compare_op=ALU.not_equal,
                                            fill=1.0, base=0, pattern=[[-2, C], [-1, 2], [0, HALF]],
                                            channel_multiplier=1).then_inc(pool_done, 1)
                    pool.wait_ge(pool_done, 4)

                @block.tensor
                def _(pe):
                    pe.wait_ge(loaded, 16 * 24)
                    for n, (source, _, _) in enumerate(turns):
                        if n >= BANKS:
                            pe.wait_ge(kept, n - BANKS + 1)
                        rows = source.shape[0]
                        nc.tensor.transpose(bank[n % BANKS][:, 0:rows], source, ident[0:rows, 0:rows]).then_inc(turned, 1)
                    pe.wait_ge(kept, len(turns))
                    pe.wait_ge(made, 1)
                    for side in range(2):
                        at = slice(side * HALF, (side + 1) * HALF)
                        if side:
                            pe.wait_ge(folded, 1)
                        for h in range(side, H, 2):
                            nc.tensor.matmul(bank[6][:, h * G:(h + 1) * G], x_rows_w[at, h // 2, :],
                                             slice_wT[at, :], start=True, stop=True)
                            last = nc.tensor.matmul(bank[7][:, h * G:(h + 1) * G], bx_wide[at, h // 2, :],
                                                    slice_wT[at, :], start=True, stop=True)
                        last.then_inc(folded, 1)

                @block.scalar
                def _(act):
                    for n, (source, to, scale) in enumerate(turns):
                        act.wait_ge(turned, n + 1)
                        rows = source.shape[0]
                        got = bank[n % BANKS][:, 0:rows]
                        if scale is None:
                            nc.scalar.copy(to, got).then_inc(kept, 1)
                        else:
                            act.wait_ge(kept, 1)
                            nc.scalar.activation(to, got, ACT.Copy, scale=scale).then_inc(kept, 1)
                    act.wait_ge(made, 2)
                    nc.scalar.activation(rate[:, :, :], log_rate[:, :, :], ACT.Exp).then_inc(kept, 1)

                @block.vector
                def _(dve):
                    steps = Chain(nc, wctx, dve, "hyw_steps", 40, w_steps)
                    steps.unit(0)
                    link = steps.link
                    nc.vector.memset(ones[:, :], 1.0)
                    dve.wait_ge(pool_done, 4)
                    nc.vector.tensor_copy(iota_f[:, :], iota_i[:, :])
                    link(nc.vector.tensor_scalar(row_m[:, :], row_i[:, :], G - 1, None, ALU.bitwise_and))
                    link(nc.vector.tensor_copy(row_f[:, :], row_m[:, :]))
                    nc.vector.tensor_scalar(later[:, :], iota_f[:, :], row_f[:, 0:1], None, ALU.is_gt)
                    link(nc.vector.tensor_scalar(earlier[:, :], iota_f[:, :], row_f[:, 0:1], None, ALU.is_lt))
                    for b in range(2):
                        nc.vector.tensor_copy(sum_later[:, b], earlier[:, :])
                        last = nc.vector.tensor_copy(sum_earlier[:, b], later[:, :])
                    link(last)
                    for b in range(2):
                        for m in (sum_later, sum_earlier):
                            last = nc.vector.memset(m[b * HALF:(b + 1) * HALF, 1 - b], 0.0)
                    link(last)
                    dve.wait_ge(loaded, 16 * 24)
                    dve.wait_ge(kept, 2)
                    for c in range(C):
                        last = nc.vector.tensor_scalar(bx_wide[:, c], ones[:, :], bx_cols[:, c:c + 1], None, ALU.mult)
                    last.then_inc(made, 1)
                    link(nc.vector.tensor_scalar(log_rate[:, :, :], log_rate[:, :, :], LOG_RATE_MAX, None, ALU.min))
                    dve.sem_inc(made, 1)
                    link(nc.vector.tensor_scalar(temp[:, :], temp[:, :], 1e-6, None, ALU.max))
                    link(nc.vector.reciprocal(cold[:, :], temp[:, :]))
                    dve.wait_ge(folded, 2)
                    by_head = lambda ap: ap.rearrange("p (h g) -> p h g", h=H)
                    wide = cold[:, :].unsqueeze(2).to_broadcast([P, H, G])
                    nc.vector.tensor_tensor(by_head(w_logit[:, :]), by_head(bank[6][:, :]), wide, ALU.mult)
                    link(nc.vector.tensor_tensor(bias_sum[:, :, :], by_head(bank[7][:, :]),
                                                 slice_b[:, :].unsqueeze(1).to_broadcast([P, H, G]), ALU.add))
                    link(nc.vector.tensor_tensor(by_head(b_logit[:, :]), bias_sum[:, :, :], wide, ALU.mult))

        x_sb = sb("x", [P, 2, QUAD, P])
        xo = sb("xo", [P, 2, QUAD, P])
        stats = sb("stats", [P, QUAD, 6])
        halves = sb("halves", [P, 3, QUAD])
        mean = sb("mean", [P, QUAD])
        var = sb("var", [P, QUAD])
        root = sb("root", [P, QUAD])
        inv = sb("inv", [P, QUAD])
        xn = sb("xn", [P, QUAD, P])
        xnT = sb("xnT", [P, QUAD, P])
        fx = sb("fx", [P, QUAD, C, P + 1])
        logit = sb("logit", [P, QUAD, H, G])
        peak = sb("peak", [P, QUAD, H])
        expo = sb("expo", [P, QUAD, H, G])
        mass = sb("mass", [P, QUAD, H])
        rmass = sb("rmass", [P, QUAD, H])
        sw = sb("sw", [P, QUAD, H, G])
        swT = sb("swT", [P, QUAD, C, P])
        snorm = sb("snorm", [P, C])
        rnorm = sb("rnorm", [P, C])
        st = sb("st", [P, 2, C, P])
        uT = sb("uT", [P, C, T])
        dt_in = sb("dt_in", [P, PAIRS, 2 * H])
        dt_abs = sb("dt_abs", [P, PAIRS, 2 * H])
        dt_exp = sb("dt_exp", [P, PAIRS, 2 * H])
        dt_s = sb("dt_s", [P, PAIRS, 2 * H])
        dt_s2 = sb("dt_s2", [P, PAIRS, 2 * H])
        dt_p = sb("dt_p", [P, PAIRS, 2 * H])
        dt = sb("dt", [P, PAIRS, 2 * H])
        decay = sb("decay", [P, PAIRS, 2 * H])
        conv = sb("conv", [P, C + 2, QUAD, G])
        xT = sb("xT", [P, C, T])
        bcT = sb("bcT", [HALF, 2, T])
        zT = sb("zT", [P, C, T])
        steps_f = sb("steps_f", [P, PAIRS, H, G])
        steps_b = sb("steps_b", [P, PAIRS, H, G])
        kept_part = sb("kept_part", [P, PAIRS, H, G])
        gram_f = sb("gram_f", [P, PAIRS, G])
        gram_b = sb("gram_b", [P, PAIRS, G])
        scan_f = sb("scan_f", [P, PAIRS, H, G])
        scan_b = sb("scan_b", [P, PAIRS, H, G])
        scanT = sb("scanT", [P, PAIRS, H, G])
        x_tok = sb("x_tok", [P, PAIRS, D])
        skip8 = sb("skip8", [H, T])
        y = sb("y", [P, C, T])
        yg = sb("yg", [P, C, T])
        ysq = sb("ysq", [P, C, QUAD, 2, G])
        ms = sb("ms", [P, QUAD])
        ms_root = sb("ms_root", [P, QUAD])
        rms = sb("rms", [P, QUAD])
        oT = sb("oT", [P, C, T])
        z_out = sb("z_out", [P, QUAD, C, P])
        summed_out = sb("summed_out", [P, QUAD, P])

        x_loaded = [sem(f"x_loaded{s}") for s in range(2)]
        names = ("x_free xo_free root_asked root_ready xn_ready xnT_in_psum xnT_ready fx_logits_in_psum fx_ready "
                 "logit_ready expo_ready sw_ready st_in_psum st_ready stT_in_psum uT_ready swT_in_psum swT_ready "
                 "dt_in_psum dt_asked dt_exp_ready decay_ready steps_ready x_in_psum conv_ready xT_ready bcT_ready "
                 "z_in_psum zT_ready gram_in_psum seg_in_psum kept_ready xtok_in_psum xtok_ready skip8_in_psum "
                 "skip8_ready skip_in_psum scan_ready y_in_psum yg_ready ysq_ready ms_in_psum ms_asked ms_root_ready "
                 "rms_ready o_in_psum oT_ready z_out_in_psum z_out_ready out_in_psum x_done ready").split()
        s = {n: sem(n) for n in names}
        init_steps, unit_steps = sem("init_steps"), sem("unit_steps")
        clear(nc, x_loaded + list(s.values()) + [init_steps, unit_steps])
        x_rows = x_in.rearrange("(g j) n f -> g n j f", j=QUAD)
        xo_rows = x_out.rearrange("(g j) n f -> g n j f", j=QUAD)

        def done(eng, name, q, u, k=1, n=1):
            eng.wait_ge(s[name], (q * 2 + u) * n + k)

        mm = nc.tensor.matmul
        tt = nc.vector.tensor_tensor
        ts = nc.vector.tensor_scalar
        stt = nc.vector.scalar_tensor_tensor
        y_bank = ((bank[0], bank[3]), (bank[6], bank[7]))
        block_of = lambda k, c: bank[k + c // 2][:, (c % 2) * T:(c % 2 + 1) * T]

        with nc.Block() as block:
            @block.sync
            def _(sp):
                with sp.Fori(0, units // 2) as q:
                    for u in range(2):
                        done(sp, "x_free", q, u)
                        sp.dma_start(x_sb[:, u], x_rows[q * 2 + u]).then_inc(x_loaded[u], 16)

            @block.gpsimd
            def _(pool):
                with pool.Fori(0, units // 2) as q:
                    for u in range(2):
                        done(pool, "decay_ready", q, u)
                        for pr in range(PAIRS):
                            for to, side, k in ((steps_f, later, 0), (steps_b, earlier, H)):
                                last = nc.gpsimd.tensor_tensor(
                                    to[:, pr], side[:, :].unsqueeze(1).to_broadcast([P, H, G]),
                                    decay[:, pr, k:k + H].unsqueeze(2).to_broadcast([P, H, G]), ALU.mult)
                            last.then_inc(s["steps_ready"], 1)
                        done(pool, "x_done", q, u)
                        pool.dma_start(xo_rows[q * 2 + u], xo[:, u]).then_inc(x_stored[u], 16)
                        pool.wait_ge(x_stored[u], q * 16 + 16)
                        pool.sem_inc(s["xo_free"], 1)

            @block.tensor
            def _(pe):
                def project(q, u, j):
                    if j >= 2:
                        done(pe, "fx_ready", q, u, j - 1, QUAD)
                        done(pe, "logit_ready", q, u, j - 1, QUAD)
                    mm(bank[1 + 2 * (j % 2)][:, :], xnT[:, j], w_fxT[:, :], start=True, stop=True)
                    mm(bank[2 + 2 * (j % 2)][:, :], xnT[:, j], w_logit[:, :], start=True,
                       stop=True).then_inc(s["fx_logits_in_psum"], 1)

                def slices(q, u, j):
                    done(pe, "fx_ready", q, u, j + 1, QUAD)
                    done(pe, "sw_ready", q, u, j + 1, QUAD)
                    flat = sw[:, j].rearrange("p h g -> p (h g)")
                    for c in range(C):
                        last = mm(bank[5 + c // 2][:, (c % 2) * (P + 1):(c % 2 + 1) * (P + 1)],
                                  flat[:, c * P:(c + 1) * P], fx[:, j, c], start=True, stop=True)
                    last.then_inc(s["st_in_psum"], 1)
                    if j:
                        done(pe, "swT_ready", q, u, j, QUAD)
                    for c in range(C):
                        last = nc.tensor.transpose(bank[0][:, c * P:(c + 1) * P], flat[:, c * P:(c + 1) * P], ident[:, :])
                    last.then_inc(s["swT_in_psum"], 1)

                def turn(q, u, j):
                    done(pe, "st_ready", q, u, j + 1, QUAD)
                    if j:
                        done(pe, "uT_ready", q, u, j, QUAD)
                    for c in range(C):
                        last = nc.tensor.transpose(bank[7][:, c * P:(c + 1) * P], st[:, j % 2, c], ident[:, :])
                    last.then_inc(s["stT_in_psum"], 1)

                with pe.Fori(0, units // 2) as q:
                    for u in range(2):
                        done(pe, "xn_ready", q, u)
                        for j in range(QUAD):
                            last = nc.tensor.transpose(bank[0][:, j * P:(j + 1) * P], xn[:, j], ident[:, :])
                        last.then_inc(s["xnT_in_psum"], 1)
                        done(pe, "xnT_ready", q, u)
                        project(q, u, 0)
                        project(q, u, 1)
                        slices(q, u, 0)
                        project(q, u, 2)
                        turn(q, u, 0)
                        slices(q, u, 1)
                        project(q, u, 3)
                        turn(q, u, 1)
                        slices(q, u, 2)
                        turn(q, u, 2)
                        slices(q, u, 3)
                        turn(q, u, 3)
                        done(pe, "uT_ready", q, u, QUAD, QUAD)
                        for pr in range(PAIRS):
                            for k in range(C):
                                last = mm(bank[6][:, pr * 2 * H:(pr + 1) * 2 * H], uT[:, k, pr * P:(pr + 1) * P],
                                          in_wT[:, k, DT:PROJ], start=(k == 0), stop=(k == C - 1))
                        last.then_inc(s["dt_in_psum"], 1)
                        for c in range(C + 2):
                            at = D + c * P if c < C else 2 * D + (c - C) * NS
                            size, to = (P, block_of(1, c)) if c < C else (NS, bank[3][0:HALF, (c - C) * T:(c - C + 1) * T])
                            for k in range(C):
                                last = mm(to, in_wT[:, k, at:at + size], uT[:, k, :], start=(k == 0), stop=(k == C - 1))
                        last.then_inc(s["x_in_psum"], 1)
                        for c in range(C):
                            for k in range(C):
                                last = mm(block_of(4, c), in_wT[:, k, c * P:(c + 1) * P], uT[:, k, :],
                                          start=(k == 0), stop=(k == C - 1))
                        last.then_inc(s["z_in_psum"], 1)
                        done(pe, "bcT_ready", q, u)
                        pe.sem_inc(s["ready"], 1)
                        for j in range(QUAD):
                            last = mm(bank[7][(j % 2) * HALF:(j % 2 + 1) * HALF, (j // 2) * G:(j // 2 + 1) * G],
                                      bcT[:, 0, j * G:(j + 1) * G], bcT[:, 1, j * G:(j + 1) * G], start=True, stop=True)
                        last.then_inc(s["gram_in_psum"], 1)
                        done(pe, "xT_ready", q, u)
                        for pr in range(PAIRS):
                            for c in range(C):
                                last = nc.tensor.transpose(bank[1 + pr][:, c * P:(c + 1) * P],
                                                           xT[:, c, pr * P:(pr + 1) * P], ident[:, :])
                            last.then_inc(s["xtok_in_psum"], 1)
                        for k in range(C):
                            last = mm(bank[3][0:H, 0:T], skip_w[:, k], xT[:, k, :], start=(k == 0), stop=(k == C - 1))
                        last.then_inc(s["skip8_in_psum"], 1)
                        done(pe, "swT_ready", q, u, QUAD, QUAD)
                        for pr in range(PAIRS):
                            done(pe, "steps_ready", q, u, pr + 1, PAIRS)
                            to = bank[6 * pr][:, :]
                            mm(to, sum_later[:, :, :], steps_f[:, pr], start=True, stop=False)
                            mm(to, sum_earlier[:, :, :], steps_b[:, pr], start=False,
                               stop=True).then_inc(s["seg_in_psum"], 1)
                        done(pe, "skip8_ready", q, u)
                        done(pe, "zT_ready", q, u)
                        for c in range(C):
                            last = mm(block_of(4, c), spread[:, c], skip8[:, :], start=True, stop=True)
                        last.then_inc(s["skip_in_psum"], 1)
                        for pr in range(PAIRS):
                            done(pe, "xtok_ready", q, u, pr + 1, PAIRS)
                            done(pe, "scan_ready", q, u, pr + 1, PAIRS)
                            pe.sem_inc(s["ready"], 1)
                            for h in range(H):
                                for b in range(2):
                                    at = slice(b * HALF, (b + 1) * HALF)
                                    last = mm(y_bank[pr][b][(h % 2) * HALF:(h % 2 + 1) * HALF,
                                                            (h // 2) * G:(h // 2 + 1) * G],
                                              x_tok[at, pr, h * HALF:(h + 1) * HALF], scanT[at, pr, h],
                                              start=True, stop=True)
                            last.then_inc(s["y_in_psum"], 1)
                        done(pe, "yg_ready", q, u)
                        for m in range(C):
                            for k in range(C):
                                last = mm(block_of(1, m), mix_w[:, k, m * P:(m + 1) * P], yg[:, k, :],
                                          start=(k == 0), stop=(k == C - 1))
                        last.then_inc(s["o_in_psum"], 1)
                        done(pe, "ysq_ready", q, u)
                        for j in range(QUAD):
                            for k in range(C):
                                last = mm(bank[7][:, j:j + 1], ysq[:, k, j].rearrange("p a g -> p (a g)"), ones[:, 0:1],
                                          start=(k == 0), stop=(k == C - 1))
                        last.then_inc(s["ms_in_psum"], 1)
                        done(pe, "oT_ready", q, u)
                        for j in range(QUAD):
                            if j >= 2:
                                done(pe, "z_out_ready", q, u, j - 1, QUAD)
                            if j == 0 or j >= 2:
                                pe.sem_inc(s["ready"], 1)
                            for h in range(H):
                                at = slice((h % 2) * HALF, (h % 2 + 1) * HALF)
                                last = mm(bank[3 + 2 * (j % 2)][at, (h // 2) * P:(h // 2 + 1) * P],
                                          oT[at, h // 2, j * G:(j + 1) * G], out_wT[at, h // 2], start=True, stop=True)
                            last.then_inc(s["z_out_in_psum"], 1)
                        for j in range(QUAD):
                            done(pe, "z_out_ready", q, u, j + 1, QUAD)
                            for c in range(C):
                                last = mm(bank[7][:, j * P:(j + 1) * P], swT[:, j, c], z_out[:, j, c],
                                          start=(c == 0), stop=(c == C - 1))
                        last.then_inc(s["out_in_psum"], 1)

            @block.scalar
            def _(act):
                def raise_(q, u, j):
                    done(act, "logit_ready", q, u, j + 1, QUAD)
                    nc.scalar.activation(expo[:, j], logit[:, j], ACT.Exp).then_inc(s["expo_ready"], 1)

                def keep_swT(q, u, j):
                    done(act, "swT_in_psum", q, u, j + 1, QUAD)
                    nc.scalar.copy(swT[:, j], bank[0][:, :]).then_inc(s["swT_ready"], 1)

                def keep_uT(q, u, j):
                    done(act, "stT_in_psum", q, u, j + 1, QUAD)
                    for b in range(2):
                        at = slice(b * HALF, (b + 1) * HALF)
                        last = nc.scalar.copy(uT[at, :, j * G:(j + 1) * G],
                                              bank[7][at, :].rearrange("p (c g) -> p c g", c=C)[:, :, b * G:(b + 1) * G])
                    last.then_inc(s["uT_ready"], 1)

                with act.Fori(0, units // 2) as q:
                    for u in range(2):
                        done(act, "root_asked", q, u)
                        nc.scalar.activation(root[:, :], var[:, :], ACT.Sqrt).then_inc(s["root_ready"], 1)
                        done(act, "xnT_in_psum", q, u)
                        nc.scalar.copy(xnT[:, :, :], bank[0][:, :]).then_inc(s["xnT_ready"], 1)
                        raise_(q, u, 0)
                        raise_(q, u, 1)
                        keep_swT(q, u, 0)
                        raise_(q, u, 2)
                        keep_uT(q, u, 0)
                        keep_swT(q, u, 1)
                        raise_(q, u, 3)
                        keep_uT(q, u, 1)
                        keep_swT(q, u, 2)
                        keep_uT(q, u, 2)
                        keep_swT(q, u, 3)
                        keep_uT(q, u, 3)
                        done(act, "dt_asked", q, u)
                        nc.scalar.activation(dt_exp[:, :, :], dt_abs[:, :, :], ACT.Exp,
                                             scale=-1.0).then_inc(s["dt_exp_ready"], 1)
                        done(act, "conv_ready", q, u)
                        nc.scalar.activation(bcT[:, :, :], conv[0:HALF, C:C + 2], ACT.Silu).then_inc(s["bcT_ready"], 1)
                        nc.scalar.activation(xT[:, :, :], conv[:, 0:C], ACT.Silu).then_inc(s["xT_ready"], 1)
                        done(act, "z_in_psum", q, u)
                        for k in range(2):
                            last = nc.scalar.activation(zT[:, 2 * k:2 * k + 2], bank[4 + k][:, :], ACT.Silu)
                        last.then_inc(s["zT_ready"], 1)
                        for pr in range(PAIRS):
                            done(act, "xtok_in_psum", q, u, pr + 1, PAIRS)
                            nc.scalar.copy(x_tok[:, pr], bank[1 + pr][:, :]).then_inc(s["xtok_ready"], 1)
                        for pr in range(PAIRS):
                            done(act, "seg_in_psum", q, u, pr + 1, PAIRS)
                            nc.scalar.activation(kept_part[:, pr], bank[6 * pr][:, :], ACT.Exp,
                                                 scale=-1.0).then_inc(s["kept_ready"], 1)
                        done(act, "yg_ready", q, u)
                        for k in range(2):
                            last = nc.scalar.activation(ysq[:, :, :, k], yg[:, :, :].rearrange("p c (j g) -> p c j g", j=QUAD), ACT.Square)
                        last.then_inc(s["ysq_ready"], 1)
                        done(act, "o_in_psum", q, u)
                        for k in range(2):
                            last = nc.scalar.copy(oT[:, 2 * k:2 * k + 2], bank[1 + k][:, :])
                        last.then_inc(s["oT_ready"], 1)
                        done(act, "ms_asked", q, u)
                        nc.scalar.activation(ms_root[:, :], ms[:, :], ACT.Sqrt).then_inc(s["ms_root_ready"], 1)
                        done(act, "rms_ready", q, u)
                        for j in range(QUAD):
                            done(act, "z_out_in_psum", q, u, j + 1, QUAD)
                            nc.scalar.activation(z_out[:, j], bank[3 + 2 * (j % 2)][:, :], ACT.Copy,
                                                 scale=rms[:, j:j + 1]).then_inc(s["z_out_ready"], 1)

            @block.vector
            def _(dve):
                init = Chain(nc, ctx, dve, "hy_init", 3, init_steps)
                init.unit(0)
                init.link(nc.vector.memset(fx[:, :, :, :], 1.0))
                init.link(nc.vector.memset(gram_f[:, :, :], 0.0))
                init.link(nc.vector.memset(gram_b[:, :, :], 0.0))
                dve.sem_inc(s["x_free"], 2)
                dve.sem_inc(s["xo_free"], 2)
                steps = Chain(nc, ctx, dve, "hy_steps", STEP_COUNT, unit_steps)
                link = steps.link
                by_head = lambda ap: ap.rearrange("p (h g) -> p h g", h=H)
                over = lambda ap: ap.unsqueeze(2).to_broadcast([P, H, G])

                def logits(q, u, j):
                    done(dve, "fx_logits_in_psum", q, u, j + 1, QUAD)
                    tt(fx[:, j, :, 0:P], bank[1 + 2 * (j % 2)][:, :].rearrange("p (c f) -> p c f", c=C),
                       b_fx[:, :].rearrange("p (c f) -> p c f", c=C), ALU.add).then_inc(s["fx_ready"], 1)
                    link(tt(logit[:, j], by_head(bank[2 + 2 * (j % 2)][:, :]), by_head(b_logit[:, :]), ALU.add))
                    link(nc.vector.tensor_reduce(peak[:, j], logit[:, j], AX_X, ALU.max))
                    tt(logit[:, j], logit[:, j], over(peak[:, j]), ALU.subtract).then_inc(s["logit_ready"], 1)

                def softmax(q, u, j):
                    done(dve, "expo_ready", q, u, j + 1, QUAD)
                    link(nc.vector.tensor_reduce(mass[:, j], expo[:, j], AX_X, ALU.add))
                    link(nc.vector.reciprocal(rmass[:, j], mass[:, j]))
                    tt(sw[:, j], expo[:, j], over(rmass[:, j]), ALU.mult).then_inc(s["sw_ready"], 1)

                def slice_tokens(q, u, j):
                    done(dve, "st_in_psum", q, u, j + 1, QUAD)
                    halves_of = lambda k: bank[5 + k][:, 0:2 * (P + 1)].rearrange("p (c f) -> p c f", c=2)
                    for k in range(2):
                        last = ts(snorm[:, 2 * k:2 * k + 2], halves_of(k)[:, :, P], 1e-5, None, ALU.add)
                    link(last)
                    link(nc.vector.reciprocal(rnorm[:, :], snorm[:, :]))
                    for k in range(2):
                        last = tt(st[:, j % 2, 2 * k:2 * k + 2], halves_of(k)[:, :, 0:P],
                                  rnorm[:, 2 * k:2 * k + 2].unsqueeze(2).to_broadcast([P, 2, P]), ALU.mult)
                    last.then_inc(s["st_ready"], 1)

                with dve.Fori(0, units // 2) as q:
                    for u in range(2):
                        steps.unit(q * 2 + u)
                        dve.wait_ge(x_loaded[u], q * 16 + 16)
                        for j in range(QUAD):
                            last = nc.vector.bn_stats(stats[:, j], x_sb[:, u, j])
                        link(last)
                        merge_statistics(nc, steps, stats[:, :], mean[:, :], var[:, :], halves[:, :])
                        ts(var[:, :], var[:, :], LN_EPS, None, ALU.add).then_inc(s["root_asked"], 1)
                        done(dve, "root_ready", q, u)
                        link(nc.vector.reciprocal(inv[:, :], root[:, :]))
                        for j in range(QUAD):
                            last = ts(xn[:, j], x_sb[:, u, j], mean[:, j:j + 1], inv[:, j:j + 1], ALU.subtract, ALU.mult)
                        last.then_inc(s["xn_ready"], 1)
                        logits(q, u, 0)
                        logits(q, u, 1)
                        softmax(q, u, 0)
                        logits(q, u, 2)
                        slice_tokens(q, u, 0)
                        softmax(q, u, 1)
                        logits(q, u, 3)
                        slice_tokens(q, u, 1)
                        softmax(q, u, 2)
                        slice_tokens(q, u, 2)
                        softmax(q, u, 3)
                        slice_tokens(q, u, 3)
                        done(dve, "dt_in_psum", q, u)
                        link(tt(dt_in[:, :, :], bank[6][:, 0:PAIRS * 2 * H].rearrange("p (a h) -> p a h", a=PAIRS),
                                dt_bias[:, :, :].rearrange("p a h -> p (a h)").unsqueeze(1).to_broadcast(
                                    [P, PAIRS, 2 * H]), ALU.add))
                        stt(out=dt_abs[:, :, :], in0=dt_in[:, :, :], scalar=-1.0, in1=dt_in[:, :, :], op0=ALU.mult,
                            op1=ALU.max).then_inc(s["dt_asked"], 1)
                        done(dve, "x_in_psum", q, u)
                        def taps(c):
                            if c < C:
                                return (conv[:, c], block_of(1, c).rearrange("p (j g) -> p j g", j=QUAD),
                                        conv_x[:, c], convb_x[:, c:c + 1])
                            return (conv[0:HALF, c], bank[3][0:HALF, (c - C) * T:(c - C + 1) * T].rearrange(
                                "p (j g) -> p j g", j=QUAD), conv_bc[:, c - C], convb_bc[:, c - C:c - C + 1])
                        for k in range(K):
                            for c in range(C + 2):
                                to, x, tap, b = taps(c)
                                tap_k = tap[:, K - 1 - k:K - k]
                                if k == 0:
                                    last = ts(to, x, tap_k, b, ALU.mult, ALU.add)
                                else:
                                    last = stt(out=to[:, :, k:G], in0=x[:, :, 0:G - k], scalar=tap_k,
                                               in1=to[:, :, k:G], op0=ALU.mult, op1=ALU.add)
                            if k < K - 1:
                                link(last)
                        last.then_inc(s["conv_ready"], 1)
                        done(dve, "dt_exp_ready", q, u)
                        link(ts(dt_s[:, :, :], dt_exp[:, :, :], 2.0, None, ALU.add))
                        link(nc.vector.reciprocal(dt_p[:, :, :], dt_s[:, :, :]))
                        link(tt(dt_s[:, :, :], dt_exp[:, :, :], dt_p[:, :, :], ALU.mult))
                        link(tt(dt_s2[:, :, :], dt_s[:, :, :], dt_s[:, :, :], ALU.mult))
                        link(ts(dt_p[:, :, :], dt_s2[:, :, :], 1.0 / (2 * SERIES + 1), None, ALU.mult))
                        for k in range(SERIES - 1, 0, -1):
                            link(stt(out=dt_p[:, :, :], in0=dt_p[:, :, :], scalar=1.0 / (2 * k + 1), in1=dt_s2[:, :, :],
                                     op0=ALU.add, op1=ALU.mult))
                        link(stt(out=dt_p[:, :, :], in0=dt_p[:, :, :], scalar=1.0, in1=dt_s[:, :, :], op0=ALU.add,
                                 op1=ALU.mult))
                        link(ts(dt_s[:, :, :], dt_in[:, :, :], 0.0, None, ALU.max))
                        link(stt(out=dt[:, :, :], in0=dt_p[:, :, :], scalar=2.0, in1=dt_s[:, :, :], op0=ALU.mult,
                                 op1=ALU.add))
                        link(tt(decay[:, :, :], dt[:, :, :], rate[:, :, :].rearrange("p a h -> p (a h)").unsqueeze(
                            1).to_broadcast([P, PAIRS, 2 * H]), ALU.mult))
                        ts(decay[:, :, :], decay[:, :, :], DECAY_MAX, None, ALU.min).then_inc(s["decay_ready"], 1)
                        done(dve, "gram_in_psum", q, u)
                        gram = bank[7][:, 0:PAIRS * G].rearrange("p (a g) -> p a g", a=PAIRS)
                        tt(gram_f[:, :, 1:G], gram[:, :, 0:G - 1],
                           later[:, 1:G].unsqueeze(1).to_broadcast([P, PAIRS, G - 1]), ALU.mult)
                        link(tt(gram_b[:, :, 0:G - 1], gram[:, :, 1:G],
                                earlier[:, 0:G - 1].unsqueeze(1).to_broadcast([P, PAIRS, G - 1]), ALU.mult))
                        done(dve, "skip8_in_psum", q, u)
                        ts(skip8[:, :], bank[3][0:H, 0:T], skip_b[:, 0:1], None, ALU.add).then_inc(s["skip8_ready"], 1)
                        for pr in range(PAIRS):
                            for to, side, k in ((scan_f, gram_f, 0), (scan_b, gram_b, H)):
                                last = tt(to[:, pr], side[:, pr].unsqueeze(1).to_broadcast([P, H, G]),
                                          over(dt[:, pr, k:k + H]), ALU.mult)
                        link(last)
                        for pr in range(PAIRS):
                            last = tt(scan_f[:, pr], scan_f[:, pr], scan_b[:, pr], ALU.add)
                        link(last)
                        for pr in range(PAIRS):
                            done(dve, "kept_ready", q, u, pr + 1, PAIRS)
                            tt(scanT[:, pr], scan_f[:, pr], kept_part[:, pr], ALU.mult).then_inc(s["scan_ready"], 1)
                        done(dve, "skip_in_psum", q, u)
                        for k in range(2):
                            last = tt(y[:, 2 * k:2 * k + 2], xT[:, 2 * k:2 * k + 2],
                                      bank[4 + k][:, :].rearrange("p (c t) -> p c t", c=2), ALU.mult)
                        link(last)
                        for pr in range(PAIRS):
                            done(dve, "y_in_psum", q, u, pr + 1, PAIRS)
                            for b in range(2):
                                at = slice(pr * P + b * G, pr * P + (b + 1) * G)
                                last = tt(y[:, :, at], y[:, :, at],
                                          y_bank[pr][b][:, 0:C * G].rearrange("p (c t) -> p c t", c=C), ALU.add)
                        link(last)
                        tt(yg[:, :, :], y[:, :, :], zT[:, :, :], ALU.mult).then_inc(s["yg_ready"], 1)
                        done(dve, "ms_in_psum", q, u)
                        ts(ms[:, :], bank[7][:, 0:QUAD], 1.0 / D, 1e-5, ALU.mult, ALU.add).then_inc(s["ms_asked"], 1)
                        done(dve, "ms_root_ready", q, u)
                        nc.vector.reciprocal(rms[:, :], ms_root[:, :]).then_inc(s["rms_ready"], 1)
                        done(dve, "out_in_psum", q, u)
                        link(tt(summed_out[:, :, :], bank[7][:, :].rearrange("p (j f) -> p j f", j=QUAD),
                                out_b[:, :].unsqueeze(1).to_broadcast([P, QUAD, P]), ALU.add))
                        done(dve, "xo_free", q, u)
                        tt(xo[:, u], summed_out[:, :, :], x_sb[:, u], ALU.add).then_inc(s["x_done"], 1)
                        done(dve, "x_done", q, u)
                        dve.sem_inc(s["x_free"], 1)
                        assert steps.k == STEP_COUNT, steps.k


STEP_COUNT = 53


def program(nc, t, out):
    graphs, nodes, features = t["x"].shape
    n_nodes = graphs * nodes
    n_edges = t["L0_ffn_edge_index"].shape[1]
    max_chunks = max_chunks_of(n_edges, n_nodes)
    dram = lambda name, shape, dt=F32: nc.dram_tensor(name, shape, dt, kind="Internal").ap()
    x1 = dram("x1", t["x"].shape)
    x2 = dram("x2", t["x"].shape)
    x3 = dram("x3", t["x"].shape)
    table = dram("table", (n_nodes, ROW))
    sorted_edges = dram("sorted_edges", (max_chunks * CHUNK, 2), I32)
    with ExitStack() as ctx:
        sb = lambda name, shape, dt=F32: ctx.enter_context(nc.sbuf_tensor(name, shape, dt))
        ident = sb("ident", [P, P])
        ident_b = sb("ident_b", [P, P], BF16)
        zeroed = ctx.enter_context(nc.semaphore("zeroed"))
        with nc.Block() as block:
            @block.gpsimd
            def _(pool):
                nc.gpsimd.memset(ident[:, :], 0.0).then_inc(zeroed, 1)
                nc.gpsimd.memset(ident_b[:, :], 0.0).then_inc(zeroed, 1)
                pool.wait_ge(zeroed, 2)
                for i in (ident, ident_b):
                    nc.gpsimd.affine_select(out=i[:, :], in_=i[:, :], compare_op=ALU.not_equal, fill=1.0,
                                            base=0, pattern=[[-1, P]], channel_multiplier=1).then_inc(zeroed, 1)
                pool.wait_ge(zeroed, 4)
        gnn_stage(nc, "g0", ident, t["x"], x1, t["adj"], t["L0_gnn_weight"], t["L0_gnn_bias"], None, True)
        with ExitStack() as gctx:
            gates = gctx.enter_context(nc.sbuf_tensor("gates", [P, graphs, EXPERTS], F32))
            with ExitStack() as actx:
                asb = lambda name, shape, dt=F32: actx.enter_context(nc.sbuf_tensor(name, shape, dt))
                chunk_block = asb("chunk_block", [1, max_chunks], I32)
                pair_count = asb("pair_count", [1, 1], I32)
                sort_stage(nc, t["L0_ffn_edge_index"], n_nodes, sorted_edges, chunk_block, pair_count)
                node_rows = asb("node_rows", [P, graphs, NODE_ROW])
                agg = asb("agg", [P, graphs, HE])
                table_stage(nc, ident, x1, t["L0_ffn_W_gat"], t["L0_ffn_att_src"], t["L0_ffn_att_dst"],
                            node_rows, table)
                attention_stage(nc, ident_b, node_rows, table, sorted_edges, chunk_block, pair_count,
                                agg[:, :, :])
                gate_stage(nc, agg[:, :, :], t["L0_ffn_b_gat"], t["L0_ffn_ln_gamma"], t["L0_ffn_ln_beta"],
                           gates[:, :, :])
            expert_stage(nc, ident, x1, x2, gates, t["L0_ffn_W1"], t["L0_ffn_b1"], t["L0_ffn_W2"], t["L0_ffn_b2"])
        gnn_stage(nc, "g1", ident, x2, x3, t["adj"], t["L1_gnn_W"], t["L1_gnn_bias"], t["L1_gnn_prelu_a"], False)
        slice_stage(nc, ident, x3, out, t)


def kernel(**inputs):
    import numpy as np
    import concourse.bacc as bacc
    from concourse.bass_utils import run_bass_kernel_spmd

    nc = bacc.Bacc("TRN2", target_bir_lowering=False, num_devices=1)
    arrays, handles = {}, {}
    for name, value in inputs.items():
        a = np.ascontiguousarray(value)
        arrays[f"in_{name}"] = a
        handles[name] = nc.dram_tensor(f"in_{name}", a.shape, mybir.dt.from_np(a.dtype), kind="ExternalInput").ap()
    out = nc.dram_tensor("out", inputs["x"].shape, F32, kind="ExternalOutput").ap()
    program(nc, handles, out)
    r = run_bass_kernel_spmd(nc, [arrays], core_ids=[0])
    return r.results[0]["out"]
```
